# Optimizing a Trainium2 kernel written in Bass

```python
import numpy as np
import jax
import jax.numpy as jnp

def _softmax(x, axis=-1):
    return jax.nn.softmax(x, axis=axis)

def _gelu(x):
    return jax.nn.gelu(x, approximate=True)

def _silu(x):
    return jax.nn.silu(x)

def _sigmoid(x):
    return jax.nn.sigmoid(x)

def _layernorm(x, axis=-1, eps=1e-05):
    m = jnp.mean(x, axis=axis, keepdims=True)
    v = jnp.var(x, axis=axis, keepdims=True)
    return (x - m) / jnp.sqrt(v + eps)

def _scatter_add(tgt, idx, src, axis=0):
    return tgt.at[idx].add(src)

def _segment_sum(src, seg, n):
    return jax.ops.segment_sum(src, seg, n)
kernel_name = 'mk_flamingo_gated_d1_seqx_r2_82c4ff'

def setup_inputs(seed: int=0):
    np.random.seed(seed)
    _w = jnp.asarray

    def _rec_inputs():
        import jax
        import jax.numpy as jnp
        _rk = jax.random.key(seed)
        x = -0.0005207 + 1.001 * jax.random.normal(jax.random.fold_in(_rk, 1), (2, 2048, 512), jnp.float32)
        _lenS = 2048 - jax.random.randint(jax.random.fold_in(_rk, 7), (2,), 0, max(1, 2048 // 4) + 1, jnp.int32)
        _lenS2 = 128 - jax.random.randint(jax.random.fold_in(_rk, 8), (2,), 0, max(1, 128 // 4) + 1, jnp.int32)
        _ctx_1024P = jax.random.normal(jax.random.fold_in(_rk, 11), (2, 16, 512), jnp.float32)
        _ctx_1024c = jax.random.dirichlet(jax.random.fold_in(_rk, 511), 0.3 * jnp.ones((16,), jnp.float32), (2, 128))
        _ctx_1024t = jnp.einsum('bsk,bkd->bsd', _ctx_1024c, _ctx_1024P)
        _ctx_1024t = _ctx_1024t * jax.lax.rsqrt(jnp.mean(jnp.square(_ctx_1024t)) + 1e-12) * 0.953939
        ctx_1024 = 4.13588e-05 + 0.999923 * (_ctx_1024t + 0.3 * jax.random.normal(jax.random.fold_in(_rk, 611), (2, 128, 512), jnp.float32))
        _validS = jnp.arange(2048)[None, :] < _lenS[:, None]
        _validS2 = jnp.arange(128)[None, :] < _lenS2[:, None]
        _causal = jnp.tril(jnp.ones((2048, 2048), dtype=bool))
        mask_BxSxS2_bk0 = jnp.logical_not(jnp.broadcast_to(_validS2[:, None, :], (2, 2048, 128)))
        _g = jax.random.normal(jax.random.fold_in(_rk, 9001), (2, 1), jnp.float32)
        _g = jnp.sign(_g) * jnp.maximum(jnp.abs(_g), 1.0) + (_g == 0) * 1.0
        g_xattn = _g[0]
        g_ffn = _g[1]
        return (x, ctx_1024, mask_BxSxS2_bk0, g_xattn, g_ffn)
    x, ctx_1024, mask_BxSxS2_bk0, g_xattn, g_ffn = _rec_inputs()

    def _L0_xattn_setup():
        import jax, jax.numpy as jnp
        import numpy as np
        NUM_HEADS = 16

        def softmax1(attn):
            padded = jnp.pad(attn, ((0, 0), (0, 0), (0, 0), (0, 1)))
            return jax.nn.softmax(padded, axis=-1)[..., :-1]
        key = jax.random.key(seed)
        ks = jax.random.split(key, 7)
        B, N, M, C = (2, 512, 2048, 512)
        x = jax.random.normal(ks[0], (B, N, C), dtype=jnp.float32)
        context = jax.random.normal(ks[1], (B, M, C), dtype=jnp.float32)
        mask = jax.random.randint(ks[2], (B, N, M), 0, 2) > 0
        s = 1.0 / np.sqrt(C)
        Wq = jax.random.normal(ks[3], (C, C), dtype=jnp.float32) * s
        Wkv = jax.random.normal(ks[4], (C, 2 * C), dtype=jnp.float32) * s
        Wproj = jax.random.normal(ks[5], (C, C), dtype=jnp.float32) * s
        bproj = jnp.zeros((C,), dtype=jnp.float32)
        return {'x': x, 'context': context, 'mask': mask, 'Wq': Wq, 'Wkv': Wkv, 'Wproj': Wproj, 'bproj': bproj}
    _L0_xattn_all = _L0_xattn_setup()
    _L0_xattn_in = {k: v for k, v in _L0_xattn_all.items() if k in ('Wq', 'Wkv', 'Wproj', 'bproj')}
    del _L0_xattn_all

    def _L0_ffn_setup():
        import jax, jax.numpy as jnp
        import numpy as np
        key = jax.random.key(seed)
        k_x, k_W, k_b, k_ids, k_w = jax.random.split(key, 5)
        N_ADAPTERS, D_OUT, D_IN = (32, 512, 512)
        B, S = (2, 1024)
        K = 8
        x = jax.random.normal(k_x, (B, S, D_IN), dtype=jnp.float32)
        W = jax.random.normal(k_W, (N_ADAPTERS, D_OUT, D_IN), dtype=jnp.float32)
        b = jax.random.normal(k_b, (N_ADAPTERS, D_OUT), dtype=jnp.float32)
        ids = jax.random.randint(k_ids, (K,), 0, N_ADAPTERS, dtype=jnp.int64)
        weights = jax.random.uniform(k_w, (K,), dtype=jnp.float32)
        return {'x': x, 'W': W, 'b': b, 'ids': ids, 'weights': weights}
    _L0_ffn_all = _L0_ffn_setup()
    _L0_ffn_in = {k: v for k, v in _L0_ffn_all.items() if k in ('W', 'b', 'ids', 'weights')}
    del _L0_ffn_all
    return {'x': x, 'ctx_1024': ctx_1024, 'mask_BxSxS2_bk0': mask_BxSxS2_bk0, 'g_xattn': g_xattn, 'g_ffn': g_ffn, 'L0_xattn_Wq': _L0_xattn_in['Wq'], 'L0_xattn_Wkv': _L0_xattn_in['Wkv'], 'L0_xattn_Wproj': _L0_xattn_in['Wproj'], 'L0_xattn_bproj': _L0_xattn_in['bproj'], 'L0_ffn_W': _L0_ffn_in['W'], 'L0_ffn_b': _L0_ffn_in['b'], 'L0_ffn_ids': _L0_ffn_in['ids'], 'L0_ffn_weights': _L0_ffn_in['weights']}

def reference(x, ctx_1024, mask_BxSxS2_bk0, g_xattn, g_ffn, L0_xattn_Wq, L0_xattn_Wkv, L0_xattn_Wproj, L0_xattn_bproj, L0_ffn_W, L0_ffn_b, L0_ffn_ids, L0_ffn_weights):
    import jax
    import jax.numpy as jnp

    def _L0_xattn_ref(x, context, mask, Wq, Wkv, Wproj, bproj):
        import jax, jax.numpy as jnp
        import numpy as np
        NUM_HEADS = 16

        def softmax1(attn):
            padded = jnp.pad(attn, ((0, 0), (0, 0), (0, 0), (0, 1)))
            return jax.nn.softmax(padded, axis=-1)[..., :-1]
        B, N, C = x.shape
        M = context.shape[1]
        H = NUM_HEADS
        d = C // H
        scale = d ** (-0.5)
        q = (x @ Wq).reshape(B, N, H, d).transpose(0, 2, 1, 3)
        kv = (context @ Wkv).reshape(B, M, 2, H, d)
        k = kv[:, :, 0].transpose(0, 2, 1, 3)
        v = kv[:, :, 1].transpose(0, 2, 1, 3)
        attn = jnp.einsum('bhnd,bhmd->bhnm', q, k) * scale
        neg = -jnp.finfo(attn.dtype).max
        attn = jnp.where(mask[:, None, :, :], neg, attn)
        attn = softmax1(attn)
        out = jnp.einsum('bhnm,bhmd->bhnd', attn, v)
        out = out.transpose(0, 2, 1, 3).reshape(B, N, C)
        return out @ Wproj + bproj

    def _L0_ffn_ref(x, W, b, ids, weights):
        import jax, jax.numpy as jnp
        import numpy as np
        Wsel = W[ids]
        bsel = b[ids]
        out = jnp.einsum('k,kod,bsd->bso', weights, Wsel, x)
        out = out + jnp.einsum('k,ko->o', weights, bsel)
        return out
    x = x + jnp.tanh(g_xattn[0]) * _L0_xattn_ref(_layernorm(x, axis=-1), ctx_1024, mask_BxSxS2_bk0, L0_xattn_Wq, L0_xattn_Wkv, L0_xattn_Wproj, L0_xattn_bproj)
    x = x + jnp.tanh(g_ffn[0]) * _L0_ffn_ref(_layernorm(x, axis=-1), L0_ffn_W, L0_ffn_b, L0_ffn_ids, L0_ffn_weights)
    return x

_drawn_inputs = setup_inputs


def setup_inputs(seed=0):
    import zlib

    import numpy as np

    out = dict(_drawn_inputs(seed))
    spreads = {'L0_xattn_bproj': (0.0, 0.1)}
    factors = {}
    for name, (base, spread) in spreads.items():
        noise = np.random.default_rng([zlib.crc32(name.encode()), seed]).standard_normal(out[name].shape)
        drawn = base * np.exp(spread * noise) if base else spread * noise
        out[name] = jnp.asarray(drawn.astype(out[name].dtype))
    for name, factor in factors.items():
        out[name] = (out[name] * factor).astype(out[name].dtype)
    return out
```

```python
from contextlib import ExitStack

import numpy as np

import concourse.bass as bass
from concourse import mybir


def flamingo_program(nc, x, ctx_in, mask, g_attn, g_ffn, wq, wkv, wproj, bproj, ffn_w, ffn_b, ids,
                     weights, const, neg, out):
    F32, F32R, BF16, U8 = mybir.dt.float32, mybir.dt.float32r, mybir.dt.bfloat16, mybir.dt.uint8
    ALU, ACT, AX = mybir.AluOpType, mybir.ActivationFunctionType, mybir.AxisListType

    P = 128
    B, N, C = x.shape
    M = ctx_in.shape[1]
    H = 16
    D = C // H
    SCALE = float(D) ** -0.5
    EPS = 1e-5
    KB = C // P
    HG = P // D
    T = 4
    TOK = T * P
    CHUNKS = B * N // TOK
    KROWS = 3 * D + 2
    NK = ids.shape[0]
    HROW = H * 2
    assert M == P and HG == 4 and KB == 4 and B == 2
    REP = 16 * 3 * HG
    ROWS = 32

    x_v = x.rearrange("b (c t p) d -> b c p t d", t=T, p=P)
    out_v = out.rearrange("b (c t p) d -> b c p t d", t=T, p=P)
    mask_v = mask.rearrange("b (c t p) m -> b c p t m", t=T, p=P)
    ffn_v = ffn_w.rearrange("a (t p) d -> a p t d", p=P)

    ctx = ExitStack()
    with ctx:
        def sb(name, shape, dt, where=ctx):
            return where.enter_context(nc.sbuf_tensor(name, shape, dt))

        def sem(name):
            return ctx.enter_context(nc.semaphore(name))

        with ExitStack() as early:
            wkv_raw = sb("wkv_raw", [P, KB, 2 * C], F32, early)
            wq_raw = sb("wq_raw", [P, KB, C], F32, early)
            wp_raw = sb("wp_raw", [P, KB, C], F32, early)
        q_stack = sb("q_stack", [P, H, TOK], F32R)
        with ExitStack() as early:
            q_hi = sb("q_hi", [P, KB, TOK], F32R, early)
            q_lo = sb("q_lo", [P, KB, TOK], F32R, early)
        probs = sb("probs", [P, 2 * HG, TOK], F32)
        with ExitStack() as early:
            w_raw = [sb(f"w_raw{i}", [P, KB, C], F32, early) for i in range(2)]
        lhs_hi = sb("lhs_hi", [P, KB, TOK], F32R)
        lhs_lo = sb("lhs_lo", [P, KB, TOK], F32R)
        with ExitStack() as early:
            w_acc = sb("w_acc", [P, KB, C], F32, early)
        scratch = sb("scratch", [P, T, C], F32)
        recip, newton, o_full = scratch[:, 0:2, :], scratch[:, 2, :], scratch[:, 3, :]
        xn_hi = sb("xn_hi", [P, KB, TOK], F32R)
        xn_lo = sb("xn_lo", [P, KB, TOK], F32R)
        xin = sb("xin", [P, T, C], F32)
        with ExitStack() as early:
            ctx_sb = sb("ctx_sb", [P, B, C], F32, early)
            ctx_t = sb("ctx_t", [P, KB, B * M], F32, early)
        xres = [sb(f"xres{i}", [P, T, C], F32) for i in range(2)]
        wq_hi = sb("wq_hi", [P, KB, C], F32R)
        wq_lo = sb("wq_lo", [P, KB, C], F32R)
        wp_hi = sb("wp_hi", [P, KB, C], F32R)
        wp_lo = sb("wp_lo", [P, KB, C], F32R)
        wf_hi = sb("wf_hi", [P, KB, C], F32R)
        wf_lo = sb("wf_lo", [P, KB, C], F32R)
        k_stack = sb("k_stack", [P, B, H, M], F32R)
        k_diag = sb("k_diag", [P, B * KB, HG * M], F32R)
        k_hi = sb("k_hi", [P, B * KB, M], F32R)
        k_lo = sb("k_lo", [P, B * KB, M], F32R)
        v_sb = sb("v_sb", [P, B, C], F32)
        bias_p = sb("bias_p", [P, C], F32)
        bias_f = sb("bias_f", [P, C], F32)
        b_raw = [sb(f"b_raw{i}", [P, C], F32) for i in range(2)]
        ident_sb = sb("ident_sb", [P, P], F32)
        ident = ident_sb[:]
        select = sb("select", [P, KB, P], F32R)
        neg_ident = sb("neg_ident", [P, P], BF16)
        ones = sb("ones", [P, D], F32)
        mask_u8 = sb("mask_u8", [P, T, M], U8)
        mask_bf = sb("mask_bf", [P, T, M], BF16)
        mask_t = sb("mask_t", [P, TOK], BF16)
        ident_bf = sb("ident_bf", [P, P], BF16)
        gates = sb("gates", [P, 2], F32)
        tanh_g = sb("tanh_g", [P, 2], F32)
        neg_tg = sb("neg_tg", [P, 1], F32)
        mix = sb("mix", [P, NK], F32)
        bn1 = sb("bn1", [P, T, 6], F32)
        mv1 = sb("mv1", [P, T, 2], F32)
        nm1 = sb("nm1", [P, T], F32)
        ve1 = sb("ve1", [P, T], F32)
        rs1 = sb("rs1", [P, T], F32)
        bn2 = sb("bn2", [P, T, 6], F32)
        mv2 = sb("mv2", [P, T, 2], F32)
        nm2 = sb("nm2", [P, T], F32)
        ve2 = sb("ve2", [P, T], F32)
        rs2 = sb("rs2", [P, T], F32)
        m_half = sb("m_half", [P, T], F32)
        max_raw = sb("max_raw", [P, T, H], F32)
        max_neg = sb("max_neg", [P, T, H], F32)
        pad_exp = sb("pad_exp", [P, T, H], F32)
        pack = sb("pack", [P, T, 4 * H], F32)
        pack_t = sb("pack_t", [2 * HROW, TOK], F32R)

        bank = [ctx.enter_context(nc.psum_tensor(f"bank{i}", [P, TOK], F32)) for i in range(8)]

        s_ident, s_select, s_const = sem("ident_in"), sem("select_in"), sem("const_in")
        s_gates, s_ctx = sem("gates_in"), sem("ctx_in")
        s_wkv, s_wq, s_wp = sem("wkv_in"), sem("wq_in"), sem("wp_in")
        s_w, s_wmix = [sem("w_in0"), sem("w_in1")], sem("w_mixed")
        x_in, res_in = sem("x_in"), [sem("res_in0"), sem("res_in1")]
        mask_in = sem("mask_in")
        setup_v, setup_a, setup_p = sem("setup_v"), sem("setup_a"), sem("setup_p")
        s_tanh, s_ctxt_mm, s_ctxt = sem("tanh_ready"), sem("ctx_t_mm"), sem("ctx_t_ready")
        s_kv_mm, s_khi, s_klo, s_v = sem("kv_mm"), sem("k_hi_ready"), sem("k_lo_ready"), sem("v_ready")
        s_kst, s_kdiag, s_kones = sem("k_stack_in"), sem("k_diag_ready"), sem("k_ones_ready")
        s_wqs, s_wph, s_wpl = sem("wq_split"), sem("wp_hi_ready"), sem("wp_lo_ready")
        s_wft_mm, s_wf = sem("wf_t_mm"), sem("wf_hi_ready")
        stat1, rstd1, xn_ready = sem("stat1"), sem("rstd1"), sem("xn_ready")
        xt_mm, xt_hi, xt_lo = sem("xt_mm"), sem("xt_hi"), sem("xt_lo")
        q_mm, qh_ready, ql_ready = sem("q_mm"), sem("qh_ready"), sem("ql_ready")
        q_copied, max_copied = sem("q_copied"), sem("max_copied")
        mx_mm, mx_read = sem("mx_mm"), sem("mx_read")
        m_neg, m_pad, m_pack = sem("m_neg"), sem("m_pad"), sem("m_pack")
        pack_mm, pack_ready = sem("pack_mm"), sem("pack_ready")
        mask_ready, maskt_mm, maskt_ready = sem("mask_ready"), sem("maskt_mm"), sem("maskt_ready")
        st_mm, exp_ready = sem("st_mm"), sem("exp_ready")
        z_mm, u_mm, ln_ready, rc_ready = sem("z_mm"), sem("u_mm"), sem("ln_ready"), sem("rc_ready")
        nt_ready, o_ready = sem("nt_ready"), sem("o_ready")
        oh_ready, ol_ready = sem("oh_ready"), sem("ol_ready")
        pj_mm, x1_ready, stat2 = sem("pj_mm"), sem("x1_ready"), sem("stat2")
        rstd2, h_ready = sem("rstd2"), sem("h_ready")
        ht_mm, ht_hi, ht_lo = sem("ht_mm"), sem("ht_hi"), sem("ht_lo")
        res_ready, x1b_ready = sem("res_ready"), sem("x1b_ready")
        ff_mm = sem("ff_mm")
        upper_read = sem("upper_read")
        stored = sem("stored")

        passed = sem("passed")

        block = ctx.enter_context(nc.Block())

        def wait_apart(engine, signal, value):
            engine.wait_ge(signal, value)
            engine.sem_inc(passed)

        def in_steps(engine, step):
            with engine.Fori(0, (CHUNKS - 2) // 2) as i:
                step(2 * i, i, 0, 2)
                step(2 * i + 1, i, 1, 2)
            step(CHUNKS - 2, (CHUNKS - 2) // 2, 0, 1)
            step(CHUNKS - 1, (CHUNKS - 2) // 2, 1, 0)

        def chunk_of(view, i, b, after):
            n = (b + after) % 2
            c = i + (b + after) // 2
            if isinstance(c, int):
                return view[n, c]
            return view[n, bass.ds(c, 1)].rearrange("o p t d -> (o p) t d")

        @block.sync
        def _(sp):
            def load_x(c, i, b, after):
                if not (isinstance(c, int) and c == 0):
                    wait_apart(sp, xt_mm, 4 * c)
                sp.dma_start(xin[:], chunk_of(x_v, i, b, after)).then_inc(x_in, 16)

            def load_res(i, b):
                sp.dma_start(xres[b][:], chunk_of(x_v, i, b, 0)).then_inc(res_in[b], 16)

            def load_mask(c, i, b, after):
                if not (isinstance(c, int) and c == 0):
                    wait_apart(sp, mask_ready, c)
                sp.dma_start(mask_u8[:], chunk_of(mask_v, i, b, after)).then_inc(mask_in, 16)

            def copy_q(c):
                sp.wait_ge(qh_ready, 4 * c + 4)
                sp.wait_ge(ql_ready, 4 * c + 4)
                stack = q_stack[:].bitcast(F32).rearrange("p (g h) n -> p g h n", h=HG)
                for block_no, part in enumerate((q_hi, q_lo, q_hi)):
                    for h in range(HG):
                        sp.dma_start(stack[D * block_no:D * block_no + D, :, h, :],
                                     part[D * h:D * h + D, :, :].bitcast(F32)).then_inc(q_copied, 16)

            def copy_max(c):
                sp.wait_ge(pack_ready, c + 1)
                for r in range(2):
                    sp.dma_start(q_stack[3 * D + r:3 * D + r + 1, :, :].bitcast(F32),
                                 pack_t[r * H:r * H + H, :].bitcast(F32)).then_inc(max_copied, 16)

            def load_adapter(k):
                a = sp.value_load(ids[k:k + 1].unsqueeze(0), min_val=0, max_val=ffn_w.shape[0] - 1)
                if k >= 2:
                    sp.wait_ge(s_wmix, 2 * (k - 1))
                sp.dma_start(w_raw[k % 2][:], ffn_v[bass.ds(a, 1)].rearrange(
                    "o p t d -> (o p) t d")).then_inc(s_w[k % 2], 16)
                sp.dma_start(b_raw[k % 2][:], ffn_b[bass.ds(a, 1), :].rearrange(
                    "o d -> (o d)").partition_broadcast(P)).then_inc(s_w[k % 2], 16)

            sp.dma_start(ident_sb[:], const[:, 0:P]).then_inc(s_ident, 16)
            sp.dma_start(ctx_sb[:], ctx_in.rearrange("b p d -> p b d")).then_inc(s_ctx, 16)
            load_x(0, 0, 0, 0)
            sp.dma_start(wkv_raw[:], wkv.rearrange("(k p) n -> p k n", p=P)).then_inc(s_wkv, 16)
            sp.dma_start(wq_raw[:], wq.rearrange("(k p) n -> p k n", p=P)).then_inc(s_wq, 16)
            sp.dma_start(gates[:, 0:1], g_attn.partition_broadcast(P)).then_inc(s_gates, 16)
            sp.dma_start(gates[:, 1:2], g_ffn.partition_broadcast(P)).then_inc(s_gates, 16)
            sp.dma_start(mix[:], weights.partition_broadcast(P)).then_inc(s_gates, 16)
            sp.dma_start(bias_p[:], bproj.partition_broadcast(P)).then_inc(s_gates, 16)
            sp.dma_start(b_raw[0][:], const[:, P:]).then_inc(s_select, 16)
            load_mask(0, 0, 0, 0)
            sp.dma_start(neg_ident[:], neg[:, 0:P]).then_inc(s_const, 16)
            sp.dma_start(ident_bf[:], neg[:, P:2 * P]).then_inc(s_const, 16)
            sp.wait_ge(setup_v, 1)
            load_adapter(0)
            load_x(1, 0, 1, 0)
            load_adapter(1)
            sp.dma_start(wp_raw[:], wproj.rearrange("(k p) n -> p k n", p=P)).then_inc(s_wp, 16)
            load_adapter(2)
            sp.wait_ge(s_khi, KB)
            sp.wait_ge(s_klo, KB)
            stack = k_stack[:].bitcast(F32).rearrange("p b (g h) m -> p (b g) h m", h=HG)
            for block_no, part in enumerate((k_hi, k_hi, k_lo)):
                for h in range(HG):
                    sp.dma_start(stack[D * block_no:D * block_no + D, :, h, :],
                                 part[D * h:D * h + D, :, :].bitcast(F32)).then_inc(s_kst, 16)
            for k in range(3, 6):
                load_adapter(k)
            sp.wait_ge(s_kv_mm, KB + B)
            sp.wait_ge(s_wpl, 1)
            copy_q(0)
            load_adapter(6)
            load_adapter(7)
            sp.wait_ge(s_v, B)
            load_res(0, 0)
            load_res(0, 1)
            copy_max(0)

            def step(s, i, b, ahead):
                if ahead >= 1:
                    load_mask(s + 1, i, b, 1)
                if ahead >= 2:
                    load_x(s + 2, i, b, 2)
                if ahead >= 1:
                    copy_q(s + 1)
                    copy_max(s + 1)
                for t in range(T):
                    wait_apart(sp, upper_read, 4 * s + 5 + t)
                    sp.dma_start(chunk_of(out_v, i, b, 0)[:, t, :], xres[b][:, t, :]).then_inc(stored, 16)
                if ahead >= 2:
                    wait_apart(sp, stored, 64 * s + 64)
                    sp.dma_start(xres[b][:], chunk_of(x_v, i, b, 2)).then_inc(res_in[b], 16)

            in_steps(sp, step)
            sp.wait_ge(stored, 64 * CHUNKS)

        @block.gpsimd
        def _(pool):
            def convert_mask(c):
                if not (isinstance(c, int) and c == 0):
                    pool.wait_ge(maskt_mm, c)
                wait_apart(pool, mask_in, 16 * c + 16)
                nc.gpsimd.tensor_copy(mask_bf[:], mask_u8[:]).then_inc(mask_ready, 1)

            def norm1(c):
                pool.wait_ge(stat1, 6 * c + 6)
                nc.gpsimd.tensor_tensor(rs1[:], ve1[:], m_half[:], ALU.pow).then_inc(rstd1, 1)
                wait_apart(pool, rstd1, c + 1)
                for t in range(T):
                    nc.gpsimd.tensor_scalar(xin[:, t, :], xin[:, t, :], nm1[:, t:t + 1],
                                            rs1[:, t:t + 1], ALU.add, ALU.mult).then_inc(xn_ready, 1)

            nc.gpsimd.memset(m_half[:], -0.5).then_inc(setup_p, 1)
            nc.gpsimd.memset(ones[:], 1.0).then_inc(setup_p, 1)
            nc.gpsimd.memset(k_diag[:].bitcast(F32), 0.0).then_inc(setup_p, 1)
            pool.wait_ge(setup_p, 3)
            norm1(0)
            convert_mask(0)
            norm1(1)

            def step(s, i, b, ahead):
                pool.wait_ge(res_in[b], 16 * i + 16)
                if b == 0:
                    pool.wait_ge(setup_v, 4)
                nc.gpsimd.tensor_tensor(xres[b][:], xres[b][:], bias_p[:].unsqueeze(1).to_broadcast(
                    [P, T, C]), ALU.add).then_inc(res_ready, 1)
                if ahead >= 1:
                    convert_mask(s + 1)
                if ahead >= 2:
                    norm1(s + 2)
                for t in range(T):
                    pool.wait_ge(stat2, 12 * s + 3 * t + 3)
                    nc.gpsimd.tensor_tensor(rs2[:, t:t + 1], ve2[:, t:t + 1], m_half[:, t:t + 1],
                                            ALU.pow).then_inc(rstd2, 1)
                    wait_apart(pool, rstd2, 4 * s + t + 1)
                    nc.gpsimd.tensor_scalar(scratch[:, t, :], xres[b][:, t, :], nm2[:, t:t + 1],
                                            rs2[:, t:t + 1], ALU.add, ALU.mult).then_inc(h_ready, 1)
                for t in range(T):
                    pool.wait_ge(h_ready, 4 * s + t + 1)
                    nc.gpsimd.tensor_tensor(xres[b][:, t, :], xres[b][:, t, :], bias_f[:],
                                            ALU.add).then_inc(x1b_ready, 1)

            in_steps(pool, step)

        @block.scalar
        def _(act):
            def xt_high(c):
                for t in range(T):
                    act.wait_ge(xt_mm, 4 * c + t + 1)
                    nc.scalar.copy(xn_hi[:, :, t * P:t * P + P],
                                   bank[t][:].rearrange("p (k n) -> p k n", k=KB)).then_inc(xt_hi, 1)

            def q_high(c):
                for g in range(KB):
                    act.wait_ge(q_mm, 4 * c + g + 1)
                    nc.scalar.copy(q_hi[:, g, :], bank[g][:]).then_inc(qh_ready, 1)

            def pad_exponential(c):
                act.wait_ge(m_neg, c + 1)
                nc.scalar.activation(pad_exp[:], max_neg[:], ACT.Exp, scale=SCALE).then_inc(m_pad, 1)

            def move_pack(c):
                act.wait_ge(pack_mm, c + 1)
                nc.scalar.copy(pack_t[:], bank[0][0:2 * HROW, :]).then_inc(pack_ready, 1)

            def move_mask(c):
                act.wait_ge(maskt_mm, c + 1)
                nc.scalar.copy(mask_t[:], bank[1][:].bitcast(BF16)[:, 0:TOK]).then_inc(maskt_ready, 1)

            act.wait_ge(s_gates, 64)
            nc.scalar.activation(tanh_g[:], gates[:], ACT.Tanh).then_inc(s_tanh, 1)
            nc.scalar.preload_act_table_set("natural_log_exp_and_others")
            for b in range(B):
                act.wait_ge(s_ctxt_mm, b + 1)
                nc.scalar.copy(ctx_t[:, :, b * M:b * M + M],
                               bank[4 + b][:].rearrange("p (k n) -> p k n", k=KB)).then_inc(s_ctxt, 1)
            xt_high(0)
            act.wait_ge(s_wq, 16)
            nc.scalar.copy(wq_hi[:], wq_raw[:]).then_inc(s_wqs, 1)
            for g in range(KB):
                act.wait_ge(s_kv_mm, g + 1)
                nc.scalar.copy(k_hi[:].rearrange("p (b g) m -> p g b m", b=B)[:, g],
                               bank[g][:, 0:B * M].rearrange("p (b m) -> p b m", b=B)).then_inc(s_khi, 1)
            q_high(0)
            act.wait_ge(setup_v, 5)
            nc.scalar.copy(wp_hi[:], wp_raw[:]).then_inc(s_wph, 1)
            for b in range(B):
                act.wait_ge(s_kv_mm, KB + b + 1)
                nc.scalar.copy(v_sb[:, b, :], bank[6 + b][:]).then_inc(s_v, 1)
            pad_exponential(0)
            xt_high(1)
            move_pack(0)
            move_mask(0)
            for k in range(KB):
                act.wait_ge(s_wft_mm, k + 1)
                nc.scalar.copy(wf_hi[:, k, :], bank[4 + k][:]).then_inc(s_wf, 1)

            def step(s, i, b, ahead):
                def exponentials(g):
                    for h in range(HG * g, HG * g + HG):
                        act.wait_ge(st_mm, 16 * s + h + 1)
                        if h % HG == 0 and g >= 2:
                            act.wait_ge(u_mm, 4 * s + g - 1)
                        nc.scalar.activation(probs[:, h % (2 * HG), :], bank[h % HG][:], ACT.Exp,
                                             scale=SCALE).then_inc(exp_ready, 1)

                def reciprocal(g):
                    act.wait_ge(z_mm, 4 * s + g + 1)
                    if g >= 2:
                        act.wait_ge(o_ready, 4 * s + g - 1)
                    nc.scalar.activation(recip[:, g % 2, :], bank[5 + 2 * (g % 2)][:],
                                         ACT.Ln).then_inc(ln_ready, 1)
                    act.wait_ge(ln_ready, 4 * s + g + 1)
                    nc.scalar.activation(recip[:, g % 2, :], recip[:, g % 2, :], ACT.Exp,
                                         scale=-1.0).then_inc(rc_ready, 1)

                exponentials(0)
                exponentials(1)
                reciprocal(0)
                exponentials(2)
                reciprocal(1)
                exponentials(3)
                reciprocal(2)
                reciprocal(3)
                if ahead >= 1:
                    q_high(s + 1)

                def high(t):
                    act.wait_ge(ht_mm, 4 * s + t + 1)
                    nc.scalar.copy(lhs_hi[:, :, t * P:t * P + P],
                                   bank[4 + t][:].rearrange("p (k n) -> p k n", k=KB)).then_inc(ht_hi, 1)
                for t in range(3):
                    high(t)
                if ahead >= 1:
                    pad_exponential(s + 1)
                if ahead >= 2:
                    xt_high(s + 2)
                high(3)
                if ahead >= 1:
                    move_pack(s + 1)
                    move_mask(s + 1)

            in_steps(act, step)

        @block.vector
        def _(dve):
            def stats1(c):
                dve.wait_ge(x_in, 16 * c + 16)
                if not (isinstance(c, int) and c == 0):
                    dve.wait_ge(xn_ready, 4 * c)
                for t in range(T):
                    nc.vector.bn_stats(bn1[:, t, :], xin[:, t, :]).then_inc(stat1, 1)
                wait_apart(dve, stat1, 6 * c + 4)
                for t in range(T):
                    last = nc.vector.bn_aggr(mv1[:, t, :], bn1[:, t, :])
                last.then_inc(stat1, 1)
                dve.wait_ge(stat1, 6 * c + 5)
                nc.vector.tensor_scalar(nm1[:], mv1[:, :, 0], -1.0, None, ALU.mult)
                nc.vector.tensor_scalar(ve1[:], mv1[:, :, 1], EPS, None, ALU.add).then_inc(stat1, 1)

            def xt_low(c):
                for t in range(T):
                    dve.wait_ge(xt_hi, 4 * c + t + 1)
                    part = slice(t * P, t * P + P)
                    nc.vector.tensor_tensor(xn_lo[:, :, part], bank[t][:].rearrange("p (k n) -> p k n", k=KB),
                                            xn_hi[:, :, part].bitcast(F32), ALU.subtract).then_inc(xt_lo, 1)

            def q_low(c):
                for g in range(KB):
                    dve.wait_ge(qh_ready, 4 * c + g + 1)
                    nc.vector.tensor_tensor(q_lo[:, g, :], bank[g][:], q_hi[:, g, :].bitcast(F32),
                                            ALU.subtract).then_inc(ql_ready, 1)

            def read_max(c, t):
                for g in range(KB):
                    dve.wait_ge(mx_mm, 16 * c + 4 * t + g + 1)
                    nc.vector.tensor_reduce(max_raw[:, t, HG * g:HG * g + HG],
                                            bank[g][:].rearrange("p (h m) -> p h m", h=HG),
                                            AX.X, ALU.max).then_inc(mx_read, 1)

            def pack_max(c):
                dve.wait_ge(mx_read, 16 * c + 16)
                nc.vector.tensor_scalar(max_neg[:], max_raw[:], -1.0, 0.0, ALU.mult,
                                        ALU.min).then_inc(m_neg, 1)
                dve.wait_ge(m_neg, c + 1)
                high, low = pack[:, :, 0:H], pack[:, :, H:2 * H]
                nc.vector.tensor_copy(high.bitcast(F32R), max_neg[:]).then_inc(m_pack, 1)
                dve.wait_ge(m_pack, 4 * c + 1)
                nc.vector.tensor_tensor(low.bitcast(F32R), max_neg[:], high, ALU.subtract).then_inc(m_pack, 1)
                dve.wait_ge(m_pad, c + 1)
                high, low = pack[:, :, 2 * H:3 * H], pack[:, :, 3 * H:4 * H]
                nc.vector.tensor_copy(high.bitcast(F32R), pad_exp[:]).then_inc(m_pack, 1)
                dve.wait_ge(m_pack, 4 * c + 3)
                nc.vector.tensor_tensor(low.bitcast(F32R), pad_exp[:], high, ALU.subtract).then_inc(m_pack, 1)

            def mix_adapter(k):
                dve.wait_ge(s_w[k % 2], 32 * (k // 2) + 32)
                if k == 0:
                    dve.wait_ge(setup_v, 3)
                    nc.vector.tensor_scalar(w_acc[:], w_raw[0][:], mix[:, 0:1], None, ALU.mult).then_inc(s_wmix, 1)
                    nc.vector.tensor_scalar(bias_f[:], b_raw[0][:], mix[:, 0:1], None, ALU.mult).then_inc(s_wmix, 1)
                    return
                dve.wait_ge(s_wmix, 2 * k)
                flat = lambda a: a[:].rearrange("p k n -> p (k n)")
                nc.vector.scalar_tensor_tensor(out=flat(w_acc), in0=flat(w_raw[k % 2]), scalar=mix[:, k:k + 1],
                                               in1=flat(w_acc), op0=ALU.mult, op1=ALU.add).then_inc(s_wmix, 1)
                nc.vector.scalar_tensor_tensor(out=bias_f[:], in0=b_raw[k % 2][:], scalar=mix[:, k:k + 1],
                                               in1=bias_f[:], op0=ALU.mult, op1=ALU.add).then_inc(s_wmix, 1)

            nc.vector.memset(k_stack[3 * D:4 * D, :, :, :].bitcast(F32), 1.0).then_inc(s_kones, 1)
            stats1(0)
            dve.wait_ge(s_select, 16)
            nc.vector.tensor_copy(select[:].rearrange("p k n -> p (k n)"), b_raw[0][:]).then_inc(setup_v, 1)
            dve.wait_ge(s_tanh, 1)
            nc.vector.tensor_scalar(neg_tg[:], tanh_g[:, 0:1], -1.0, None, ALU.mult).then_inc(setup_v, 1)
            nc.vector.tensor_scalar(mix[:], mix[:], tanh_g[:, 1:2], None, ALU.mult).then_inc(setup_v, 1)
            nc.vector.tensor_scalar(bias_p[:], bias_p[:], tanh_g[:, 0:1], None, ALU.mult).then_inc(setup_v, 1)
            xt_low(0)
            dve.wait_ge(s_wqs, 1)
            nc.vector.tensor_tensor(wq_lo[:], wq_raw[:], wq_hi[:].bitcast(F32), ALU.subtract).then_inc(s_wqs, 1)
            mix_adapter(0)
            dve.wait_ge(setup_p, 3)
            for g in range(KB):
                dve.wait_ge(s_khi, g + 1)
                nc.vector.tensor_tensor(k_lo[:].rearrange("p (b g) m -> p g b m", b=B)[:, g],
                                        bank[g][:, 0:B * M].rearrange("p (b m) -> p b m", b=B),
                                        k_hi[:].bitcast(F32).rearrange("p (b g) m -> p g b m", b=B)[:, g],
                                        ALU.subtract).then_inc(s_klo, 1)
            for h in range(HG):
                rows = slice(D * h, D * h + D)
                last = nc.vector.tensor_copy(k_diag[rows, :, h * M:h * M + M], k_hi[rows, :, :].bitcast(F32))
            last.then_inc(s_kdiag, 1)
            mix_adapter(1)
            mix_adapter(2)
            q_low(0)
            dve.wait_ge(s_wp, 16)
            dve.wait_ge(setup_v, 2)
            nc.vector.tensor_scalar(wp_raw[:], wp_raw[:], neg_tg[:], None, ALU.mult).then_inc(setup_v, 1)
            read_max(0, 0)
            dve.wait_ge(s_wph, 1)
            nc.vector.tensor_tensor(wp_lo[:], wp_raw[:], wp_hi[:].bitcast(F32), ALU.subtract).then_inc(s_wpl, 1)
            mix_adapter(3)
            read_max(0, 1)
            mix_adapter(4)
            read_max(0, 2)
            mix_adapter(5)
            read_max(0, 3)
            pack_max(0)
            stats1(1)
            mix_adapter(6)
            xt_low(1)
            mix_adapter(7)
            for k in range(KB):
                dve.wait_ge(s_wf, k + 1)
                nc.vector.tensor_tensor(wf_lo[:, k, :], bank[4 + k][:], wf_hi[:, k, :].bitcast(F32),
                                        ALU.subtract).then_inc(upper_read, 1)

            def step(s, i, b, ahead):
                def newton_step(g):
                    z, u = bank[5 + 2 * (g % 2)], bank[4 + 2 * (g % 2)]
                    r = recip[:, g % 2, :]
                    dve.wait_ge(rc_ready, 4 * s + g + 1)
                    nc.vector.tensor_tensor(newton, z[:], r, ALU.mult).then_inc(nt_ready, 1)
                    dve.wait_ge(nt_ready, 8 * s + 2 * g + 1)
                    nc.vector.scalar_tensor_tensor(out=r, in0=newton, scalar=2.0, in1=r,
                                                   op0=ALU.subtract, op1=ALU.mult).then_inc(nt_ready, 1)
                    dve.wait_ge(nt_ready, 8 * s + 2 * g + 2)
                    dve.wait_ge(u_mm, 4 * s + g + 1)
                    nc.vector.tensor_tensor(o_full, u[:], r, ALU.mult).then_inc(o_ready, 1)
                    dve.wait_ge(o_ready, 4 * s + g + 1)
                    nc.vector.tensor_copy(lhs_hi[:, g, :], o_full).then_inc(oh_ready, 1)
                    dve.wait_ge(oh_ready, 4 * s + g + 1)
                    nc.vector.tensor_tensor(lhs_lo[:, g, :], o_full, lhs_hi[:, g, :].bitcast(F32),
                                            ALU.subtract).then_inc(ol_ready, 1)

                for g in range(KB):
                    newton_step(g)
                if ahead >= 2:
                    stats1(s + 2)
                if ahead >= 1:
                    q_low(s + 1)
                dve.wait_ge(res_ready, s + 1)
                for t in range(T):
                    dve.wait_ge(pj_mm, 4 * s + t + 1)
                    nc.vector.tensor_tensor(xres[b][:, t, :], bank[4 + t][:], xres[b][:, t, :],
                                            ALU.add).then_inc(x1_ready, 1)
                    dve.wait_ge(x1_ready, 4 * s + t + 1)
                    nc.vector.bn_stats(bn2[:, t, :], xres[b][:, t, :]).then_inc(stat2, 1)
                    wait_apart(dve, stat2, 12 * s + 3 * t + 1)
                    nc.vector.bn_aggr(mv2[:, t, :], bn2[:, t, :]).then_inc(stat2, 1)
                    dve.wait_ge(stat2, 12 * s + 3 * t + 2)
                    nc.vector.tensor_scalar(nm2[:, t:t + 1], mv2[:, t, 0:1], -1.0, None, ALU.mult)
                    nc.vector.tensor_scalar(ve2[:, t:t + 1], mv2[:, t, 1:2], EPS, None,
                                            ALU.add).then_inc(stat2, 1)
                    if ahead >= 1:
                        read_max(s + 1, t)

                def h_low(t):
                    dve.wait_ge(ht_hi, 4 * s + t + 1)
                    part = slice(t * P, t * P + P)
                    nc.vector.tensor_tensor(lhs_lo[:, :, part], bank[4 + t][:].rearrange("p (k n) -> p k n", k=KB),
                                            lhs_hi[:, :, part].bitcast(F32), ALU.subtract).then_inc(ht_lo, 1)

                for t in range(3):
                    h_low(t)
                if ahead >= 1:
                    pack_max(s + 1)
                if ahead >= 2:
                    xt_low(s + 2)
                h_low(3)
                for t in range(T):
                    dve.wait_ge(ff_mm, 4 * s + t + 1)
                    dve.wait_ge(x1b_ready, 4 * s + t + 1)
                    nc.vector.tensor_tensor(xres[b][:, t, :], bank[4 + t][:], xres[b][:, t, :],
                                            ALU.add).then_inc(upper_read, 1)

            in_steps(dve, step)

        @block.tensor
        def _(pe):
            mm = nc.tensor.matmul

            def split_product(dst, lhs_h, lhs_l, rhs_h, rhs_l):
                for k in range(KB):
                    mm(dst, lhs_h(k), rhs_h(k), start=(k == 0), stop=False)
                    mm(dst, lhs_h(k), rhs_l(k), start=False, stop=False)
                    last = mm(dst, lhs_l(k), rhs_h(k), start=False, stop=(k == KB - 1))
                return last

            def transpose_x(c, first_bank_wait):
                for t in range(T):
                    first_bank_wait(t)
                    pe.wait_ge(xn_ready, 4 * c + t + 1)
                    for k in range(KB):
                        last = nc.tensor.transpose(bank[t][:, k * P:k * P + P], xin[:, t, k * P:k * P + P], ident)
                    last.then_inc(xt_mm, 1)

            def queries(c):
                pe.wait_ge(xt_hi, 4 * c + 4)
                pe.wait_ge(xt_lo, 4 * c + 4)
                for g in range(KB):
                    cols = slice(g * P, g * P + P)
                    split_product(bank[g][:], lambda k: wq_hi[:, k, cols], lambda k: wq_lo[:, k, cols],
                                  lambda k: xn_hi[:, k, :], lambda k: xn_lo[:, k, :]).then_inc(q_mm, 1)

            def scores_for_max(c, b, t):
                for g in range(KB):
                    if t == 0:
                        pe.wait_ge(ql_ready, 4 * c + g + 1)
                    else:
                        pe.wait_ge(mx_read, 16 * c + 4 * (t - 1) + g + 1)
                    mm(bank[g][:].rearrange("p (h m) -> p h m", h=HG), neg_ident[:],
                       mask_bf[:, t:t + 1, :].to_broadcast([P, HG, M]), start=True, stop=False)
                    mm(bank[g][:], q_hi[:, g, t * P:t * P + P], k_diag[:, b * KB + g, :],
                       start=False, stop=True).then_inc(mx_mm, 1)

            def transpose_pack(c):
                wait_apart(pe, m_pack, 4 * c + 4)
                for t in range(T):
                    last = nc.tensor.transpose(bank[0][0:2 * HROW, t * P:t * P + P], pack[:, t, :], ident)
                last.then_inc(pack_mm, 1)

            def transpose_mask(c):
                for t in range(T):
                    last = nc.tensor.transpose(bank[1][:].bitcast(BF16)[:, t * P:t * P + P], mask_bf[:, t, :],
                                               ident_bf[:])
                last.then_inc(maskt_mm, 1)

            pe.wait_ge(s_ident, 16)
            pe.wait_ge(s_ctx, 16)
            for b in range(B):
                for k in range(KB):
                    last = nc.tensor.transpose(bank[4 + b][:, k * P:k * P + P], ctx_sb[:, b, k * P:k * P + P], ident)
                last.then_inc(s_ctxt_mm, 1)
            transpose_x(0, lambda t: None)
            pe.wait_ge(s_wkv, 16)
            pe.wait_ge(s_ctxt, B)
            for g in range(KB):
                pe.wait_ge(xt_lo, g + 1)
                for k in range(KB):
                    last = mm(bank[g][:, 0:B * M], wkv_raw[:, k, g * P:g * P + P], ctx_t[:, k, :],
                              start=(k == 0), stop=(k == KB - 1))
                last.then_inc(s_kv_mm, 1)
            pe.wait_ge(s_wqs, 2)
            pe.wait_ge(s_klo, KB)
            queries(0)

            def values(b):
                for k in range(KB):
                    last = mm(bank[6 + b][:], ctx_t[:, k, b * M:b * M + M], wkv_raw[:, k, C:2 * C],
                              start=(k == 0), stop=(k == KB - 1))
                last.then_inc(s_kv_mm, 1)

            pe.wait_ge(s_kdiag, 1)
            pe.wait_ge(s_const, 32)
            pe.wait_ge(mask_ready, 1)
            scores_for_max(0, 0, 0)
            values(0)
            scores_for_max(0, 0, 1)
            values(1)
            scores_for_max(0, 0, 2)
            scores_for_max(0, 0, 3)
            transpose_x(1, lambda t: pe.wait_ge(mx_read, 13 + t))
            pe.wait_ge(xt_lo, 8)
            transpose_pack(0)
            transpose_mask(0)
            pe.wait_ge(s_wmix, 2 * NK)
            pe.wait_ge(s_v, B)
            for k in range(KB):
                for o in range(KB):
                    last = nc.tensor.transpose(bank[4 + k][:, o * P:o * P + P], w_acc[:, o, k * P:k * P + P], ident)
                last.then_inc(s_wft_mm, 1)
            pe.wait_ge(s_kst, 16 * 3 * HG)
            pe.wait_ge(setup_p, 3)
            pe.wait_ge(s_kones, 1)
            pe.wait_ge(setup_v, 1)

            def step(s, i, b, ahead):
                def scores(g):
                    for h in range(HG * g, HG * g + HG):
                        dst = bank[h % HG][:]
                        if g >= 1:
                            pe.wait_ge(exp_ready, 16 * s + h - HG + 1)
                        mm(dst, neg_ident[:], mask_t[:], start=True, stop=False)
                        mm(dst, k_stack[0:KROWS, b, h, :], q_stack[0:KROWS, h, :], start=False,
                           stop=True).then_inc(st_mm, 1)

                def products(g):
                    u, z = bank[4 + 2 * (g % 2)], bank[5 + 2 * (g % 2)]
                    if g == 0:
                        pe.wait_ge(upper_read, 4 * s + 4)
                    if g >= 2:
                        pe.wait_ge(o_ready, 4 * s + g - 1)
                    mm(z[:], select[HROW:2 * HROW, g, :], pack_t[HROW:2 * HROW, :], start=True, stop=True)
                    pe.wait_ge(exp_ready, 16 * s + HG * g + HG)
                    for j in range(HG):
                        last = mm(z[D * j:D * j + D, :], ones[:], probs[:, (HG * g + j) % (2 * HG), :],
                                  start=False, stop=True, skip_group_check=True)
                    last.then_inc(z_mm, 1)
                    for j in range(HG):
                        h = HG * g + j
                        last = mm(u[D * j:D * j + D, :], v_sb[:, b, D * h:D * h + D], probs[:, h % (2 * HG), :],
                                  start=True, stop=True)
                    last.then_inc(u_mm, 1)

                pe.wait_ge(q_copied, REP * s + REP)
                pe.wait_ge(max_copied, ROWS * s + ROWS)
                pe.wait_ge(maskt_ready, s + 1)
                if ahead >= 1:
                    pe.wait_ge(xt_lo, 4 * s + 8)
                scores(0)
                scores(1)
                products(0)
                scores(2)
                products(1)
                scores(3)
                products(2)
                products(3)
                if ahead >= 1:
                    pe.wait_ge(exp_ready, 16 * s + 16)
                    queries(s + 1)
                    pe.wait_ge(mask_ready, s + 2)
                pe.wait_ge(ol_ready, 4 * s + 4)
                pe.wait_ge(s_wpl, 1)
                for t in range(T):
                    part = slice(t * P, t * P + P)
                    split_product(bank[4 + t][:], lambda k: lhs_hi[:, k, part], lambda k: lhs_lo[:, k, part],
                                  lambda k: wp_hi[:, k, :], lambda k: wp_lo[:, k, :]).then_inc(pj_mm, 1)
                    if ahead >= 1:
                        scores_for_max(s + 1, 1 - b, t)
                def transpose_h(t):
                    pe.wait_ge(h_ready, 4 * s + t + 1)
                    for k in range(KB):
                        last = nc.tensor.transpose(bank[4 + t][:, k * P:k * P + P], scratch[:, t, k * P:k * P + P],
                                                   ident)
                    last.then_inc(ht_mm, 1)

                def ffn(t):
                    part = slice(t * P, t * P + P)
                    pe.wait_ge(ht_lo, 4 * s + t + 1)
                    split_product(bank[4 + t][:], lambda k: lhs_hi[:, k, part], lambda k: lhs_lo[:, k, part],
                                  lambda k: wf_hi[:, k, :], lambda k: wf_lo[:, k, :]).then_inc(ff_mm, 1)

                for t in range(3):
                    transpose_h(t)
                if ahead >= 2:
                    transpose_x(s + 2, lambda t: pe.wait_ge(mx_read, 16 * s + 29 + t))
                ffn(0)
                transpose_h(3)
                if ahead >= 1:
                    if ahead >= 2:
                        pe.wait_ge(xt_lo, 4 * s + 12)
                    transpose_pack(s + 1)
                    transpose_mask(s + 1)
                for t in range(1, T):
                    ffn(t)

            in_steps(pe, step)


_INS = ['x', 'ctx_1024', 'mask_BxSxS2_bk0', 'g_xattn', 'g_ffn', 'L0_xattn_Wq', 'L0_xattn_Wkv',
        'L0_xattn_Wproj', 'L0_xattn_bproj', 'L0_ffn_W', 'L0_ffn_b', 'L0_ffn_ids', 'L0_ffn_weights']


def kernel(**inputs):
    import ml_dtypes
    import concourse.bacc as bacc
    from concourse.bass_utils import run_bass_kernel_spmd

    nc = bacc.Bacc("TRN2", target_bir_lowering=False, num_devices=1, dynamic_dma_scratch_size=64)
    arrays, args = {}, []

    def add(name, a):
        arrays[name] = a
        args.append(nc.dram_tensor(name, a.shape, mybir.dt.from_np(a.dtype), kind="ExternalInput").ap())

    for name in _INS:
        a = np.ascontiguousarray(inputs[name])
        add(f"in_{name}", a)
    p, heads, d, groups = 128, 16, 32, 4
    const = np.zeros((p, p + groups * p), np.float32)
    const[:, :p] = np.eye(p)
    for row in range(2 * heads):
        h = row % heads
        at = p + (h // 4) * p + (h % 4) * d
        const[2 * heads + row, at:at + d] = 1.0
    add("const_f32", const)
    neg = np.concatenate([np.eye(p) * -1e38, np.eye(p)], axis=1).astype(ml_dtypes.bfloat16)
    add("const_bf16", neg)
    shape = inputs['x'].shape
    args.append(nc.dram_tensor("out_0", shape, mybir.dt.float32, kind="ExternalOutput").ap())
    flamingo_program(nc, *args)
    r = run_bass_kernel_spmd(nc, [arrays], core_ids=[0])
    return r.results[0]["out_0"]
```

```python
from contextlib import ExitStack

import numpy as np

import concourse.bass as bass
from concourse import mybir


def flamingo_program(nc, x, ctx_in, mask, g_attn, g_ffn, wq, wkv, wproj, bproj, ffn_w, ffn_b, ids,
                     weights, eye, out):
    F32, F32R, BF16, U8 = mybir.dt.float32, mybir.dt.float32r, mybir.dt.bfloat16, mybir.dt.uint8
    ALU, ACT = mybir.AluOpType, mybir.ActivationFunctionType

    P = 128
    B, N, C = x.shape
    M = ctx_in.shape[1]
    H = 16
    D = C // H
    SCALE = float(D) ** -0.5
    MASKED = -1e38
    EPS = 1e-5
    KB = C // P
    HG = P // D
    T = 4
    TOK = T * P
    CHUNKS = B * N // TOK
    UNITS = KB * T
    LAST, AT_END = CHUNKS - 1, (CHUNKS - 1) % 2
    KROWS = 3 * D
    NK = ids.shape[0]
    REP = 16 * 3
    assert NK == 2 * KB
    assert M == P and HG == 4 and KB == 4 and B == 2 and CHUNKS % 2 == 0

    x_v = x.rearrange("b (c t p) d -> b c p t d", t=T, p=P)
    out_v = out.rearrange("b (c t p) d -> b c p t d", t=T, p=P)
    mask_v = mask.rearrange("b (c t p) m -> b c p t m", t=T, p=P)
    ffn_v = ffn_w.rearrange("a (t p) d -> a p t d", p=P)

    ctx = ExitStack()
    with ctx:
        def sb(name, shape, dt, where=ctx):
            return where.enter_context(nc.sbuf_tensor(name, shape, dt))

        def sem(name):
            return ctx.enter_context(nc.semaphore(name))

        with ExitStack() as early:
            wq_raw = sb("wq_raw", [P, KB, C], F32, early)
        q_stack = sb("q_stack", [P, H, TOK], F32R)
        with ExitStack() as early:
            wkv_raw = sb("wkv_raw", [P, KB, 2 * C], F32, early)
        o_hi, o_lo = [None, None], [None, None]
        o_hi[0] = sb("o_hi0", [P, KB, TOK], F32R)
        o_lo[0] = sb("o_lo0", [P, KB, TOK], F32R)
        with ExitStack() as early:
            w_raw = [sb(f"w_raw{i}", [P, KB, C], F32, early) for i in range(2)]
        o_hi[1] = sb("o_hi1", [P, KB, TOK], F32R)
        o_lo[1] = sb("o_lo1", [P, KB, TOK], F32R)
        with ExitStack() as early:
            w_acc = sb("w_acc", [P, KB, C], F32, early)
        h_hi = [sb(f"h_hi{i}", [P, KB, P], F32R) for i in range(2)]
        h_lo = [sb(f"h_lo{i}", [P, KB, P], F32R) for i in range(2)]
        with ExitStack() as early:
            ctx_sb = sb("ctx_sb", [P, B, C], F32, early)
            ctx_t = sb("ctx_t", [P, KB, B * M], F32, early)
            wp_raw = sb("wp_raw", [P, KB, C], F32, early)
        xres = [sb(f"xres{i}", [P, T, C], F32) for i in range(2)]
        xn_hi = sb("xn_hi", [P, KB, TOK], F32R)
        xn_lo = sb("xn_lo", [P, KB, TOK], F32R)
        xin = sb("xin", [P, T, C], F32)
        x1n = [sb(f"x1n{i}", [P, C], F32) for i in range(2)]
        wq_hi = sb("wq_hi", [P, KB, C], F32R)
        wq_lo = sb("wq_lo", [P, KB, C], F32R)
        wp_hi = sb("wp_hi", [P, KB, C], F32R)
        wp_lo = sb("wp_lo", [P, KB, C], F32R)
        with ExitStack() as early:
            wk_sb = sb("wk_sb", [P, KB, C], F32, early)
        wf_hi = sb("wf_hi", [P, KB, C], F32R)
        wf_lo = sb("wf_lo", [P, KB, C], F32R)
        k_stack = sb("k_stack", [P, HG, B * KB, M], F32R)
        v_sb = sb("v_sb", [P, B, C], F32)
        bias_p = sb("bias_p", [P, C], F32)
        bias_f = sb("bias_f", [P, C], F32)
        with ExitStack() as early:
            k_hi = sb("k_hi", [P, B * KB, M], F32R, early)
            k_lo = sb("k_lo", [P, B * KB, M], F32R, early)
        probs = [sb(f"probs{i}", [P, HG, M + 1], F32) for i in range(4)]
        b_raw = [sb(f"b_raw{i}", [P, C], F32) for i in range(2)]
        q_hi = [sb(f"q_hi{i}", [P, TOK], F32R) for i in range(2)]
        q_lo = [sb(f"q_lo{i}", [P, TOK], F32R) for i in range(2)]
        scores = [sb(f"scores{i}", [P, HG, M + 1], F32) for i in range(2)]
        probs_t = [sb(f"probs_t{i}", [P, HG, P], F32) for i in range(2)]
        neg_max = sb("neg_max", [P, 4, HG], F32)
        z_sum = sb("z_sum", [P, 4, HG], F32)
        z_inv = sb("z_inv", [P, 4, HG], F32)
        ident_sb = sb("ident_sb", [P, P], F32)
        ident = ident_sb[:]
        mask_u8 = sb("mask_u8", [P, T, M], U8)
        mask_bf = [sb(f"mask_bf{i}", [P, T, M], BF16) for i in range(2)]
        gates = sb("gates", [P, 2], F32)
        tanh_g = sb("tanh_g", [P, 2], F32)
        mix = sb("mix", [P, NK], F32)
        bn1 = sb("bn1", [P, T, 6], F32)
        mv1 = sb("mv1", [P, T, 2], F32)
        nm1 = sb("nm1", [P, T], F32)
        ve1 = sb("ve1", [P, T], F32)
        rs1 = sb("rs1", [P, T], F32)
        bn2 = sb("bn2", [P, T, 6], F32)
        mv2 = sb("mv2", [P, T, 2], F32)
        nm2 = sb("nm2", [P, T], F32)
        ve2 = sb("ve2", [P, T], F32)
        rs2 = sb("rs2", [P, T], F32)
        m_half = sb("m_half", [P, T], F32)

        bank = [ctx.enter_context(nc.psum_tensor(f"bank{i}", [P, TOK], F32)) for i in range(8)]
        S_BANK, PT_BANK, O_BANK = (0, 1), (2, 3), 4
        PROJ_BANK, Q_BANK, FFN_BANK = 5, 6, 7
        LAST_PROJ_BANKS, LAST_FFN_BANKS = (5, 0, 1, 2), (7, 6, 3, 4)
        XT_BANKS = (6, 7, 6, 7)
        WF_BANKS = (5, 7, 5, 7)

        s_ident, s_gates, s_ctx = sem("ident_in"), sem("gates_in"), sem("ctx_in")
        s_wkv, s_wq, s_wp, s_wk = sem("wkv_in"), sem("wq_in"), sem("wp_in"), sem("wk_ready")
        s_w, s_wmix = [sem("w_in0"), sem("w_in1")], sem("w_mixed")
        x_in, mask_in = sem("x_in"), sem("mask_in")
        res_in = [sem("res_in0"), sem("res_in1")]
        setup_v, setup_p = sem("setup_v"), sem("setup_p")
        s_tanh, s_ctxt_mm, s_ctxt = sem("tanh_ready"), sem("ctx_t_mm"), sem("ctx_t_ready")
        s_k_mm, s_v_mm, s_v = sem("k_mm"), sem("v_mm"), sem("v_ready")
        s_khi, s_klo, s_kst = sem("k_hi_ready"), sem("k_lo_ready"), sem("k_stack_in")
        s_wqs, s_wph, s_wpl = sem("wq_split"), sem("wp_hi_ready"), sem("wp_lo_ready")
        s_wft_mm, s_wf = sem("wf_t_mm"), sem("wf_hi_ready")
        stat1, rstd1, xn_ready = sem("stat1"), sem("rstd1"), sem("xn_ready")
        xt_mm, xt_hi, xt_lo = sem("xt_mm"), sem("xt_hi"), sem("xt_lo")
        q_mm, qh_ready, ql_ready = sem("q_mm"), sem("qh_ready"), sem("ql_ready")
        q_in = [sem(f"q_in{g}") for g in range(KB)]
        mask_ready = sem("mask_ready")
        st_mm, st_read, exp_ready = sem("st_mm"), sem("st_read"), sem("exp_ready")
        inv_ready, norm_ready = sem("inv_ready"), sem("norm_ready")
        pt_mm, pt_ready, u_mm = sem("pt_mm"), sem("pt_ready"), sem("u_mm")
        oh_ready, ol_ready = sem("oh_ready"), sem("ol_ready")
        res_ready = sem("res_ready")
        pj_mm, x1_ready, stat2 = sem("pj_mm"), sem("x1_ready"), sem("stat2")
        rstd2, h_ready, x1b_ready = sem("rstd2"), sem("h_ready"), sem("x1b_ready")
        ht_mm, ht_hi, ht_lo = sem("ht_mm"), sem("ht_hi"), sem("ht_lo")
        ff_mm, ffn_bank_read = sem("ff_mm"), sem("ffn_bank_read")
        stored = sem("stored")
        passed = sem("passed")

        block = ctx.enter_context(nc.Block())

        def wait_apart(engine, signal, value):
            engine.wait_ge(signal, value)
            engine.sem_inc(passed)

        def by_channel(a):
            return a.rearrange("p k (g d h) -> p (k g) h d", h=HG, d=D)

        def in_steps(engine, step):
            loops = (CHUNKS - 4) // 2
            step(0, 0, before=False)
            with engine.Fori(0, loops) as i:
                step(i, 1)
                step(i, 2)
            step(loops, 1)
            step(loops, 2, ahead=False)
            step(loops + 1, 1, after=False, ahead=False)

        def in_range(j, before, after):
            return before if j < 0 else j < UNITS or after

        def chunk_of(view, i, k):
            c = i + k // 2
            if isinstance(c, int):
                return view[k % 2, c]
            return view[k % 2, bass.ds(c, 1)].rearrange("o p t d -> (o p) t d")

        @block.sync
        def _(sp):
            def load_x(i, k):
                sp.dma_start(xin[:], chunk_of(x_v, i, k)).then_inc(x_in, 16)

            def load_mask(i, k):
                sp.dma_start(mask_u8[:], chunk_of(mask_v, i, k)).then_inc(mask_in, 16)

            def load_res(i, k):
                sp.dma_start(xres[k % 2][:], chunk_of(x_v, i, k)).then_inc(res_in[k % 2], 16)

            def copy_q(c, g):
                wait_apart(sp, qh_ready, 4 * c + g + 1)
                wait_apart(sp, ql_ready, 4 * c + g + 1)
                for block_no, part in enumerate((q_hi, q_lo, q_hi)):
                    sp.dma_start(q_stack[D * block_no:D * block_no + D, HG * g:HG * g + HG, :].bitcast(F32),
                                 part[g % 2][:].bitcast(F32)).then_inc(q_in[g], 16)

            def load_adapter(k):
                a = sp.value_load(ids[k:k + 1].unsqueeze(0), min_val=0, max_val=ffn_w.shape[0] - 1)
                if k >= 2:
                    sp.wait_ge(s_wmix, 2 * (k - 1))
                sp.dma_start(w_raw[k % 2][:], ffn_v[bass.ds(a, 1)].rearrange(
                    "o p t d -> (o p) t d")).then_inc(s_w[k % 2], 16)
                sp.dma_start(b_raw[k % 2][:], ffn_b[bass.ds(a, 1), :].rearrange(
                    "o d -> (o d)").partition_broadcast(P)).then_inc(s_w[k % 2], 16)

            sp.dma_start(ident_sb[:], eye[:, :]).then_inc(s_ident, 16)
            sp.dma_start(ctx_sb[:], ctx_in.rearrange("b p d -> p b d")).then_inc(s_ctx, 16)
            load_x(0, 0)
            sp.dma_start(wkv_raw[:], wkv.rearrange("(k p) n -> p k n", p=P)).then_inc(s_wkv, 16)
            sp.dma_start(wq_raw[:], wq.rearrange("(k p) n -> p k n", p=P)).then_inc(s_wq, 16)
            load_mask(0, 0)
            sp.dma_start(gates[:, 0:1], g_attn.partition_broadcast(P)).then_inc(s_gates, 16)
            sp.dma_start(gates[:, 1:2], g_ffn.partition_broadcast(P)).then_inc(s_gates, 16)
            sp.dma_start(mix[:], weights.partition_broadcast(P)).then_inc(s_gates, 16)
            sp.dma_start(bias_p[:], bproj.partition_broadcast(P)).then_inc(s_gates, 16)
            sp.dma_start(wp_raw[:], wproj.rearrange("(k p) n -> p k n", p=P)).then_inc(s_wp, 16)
            sp.wait_ge(mask_ready, 1)
            load_mask(0, 1)
            sp.wait_ge(xt_mm, 4)
            load_x(0, 1)
            load_adapter(0)
            load_adapter(1)
            sp.wait_ge(s_khi, KB)
            sp.wait_ge(s_klo, KB)
            for block_no, part in enumerate((k_hi, k_hi, k_lo)):
                sp.dma_start(k_stack[D * block_no:D * block_no + D, :, :, :].bitcast(F32),
                             part[:].bitcast(F32)).then_inc(s_kst, 16)
            sp.wait_ge(s_wqs, 2)
            for g in range(KB):
                copy_q(0, g)
            load_adapter(2)
            load_adapter(3)
            sp.wait_ge(s_v, B)
            load_res(0, 0)
            sp.wait_ge(s_wpl, 1)
            load_res(0, 1)

            def step(i, k, before=True, after=True, ahead=True):
                s = 2 * i + k
                for g in range(KB):
                    if g == 0 and ahead:
                        wait_apart(sp, xt_mm, 4 * s + 8)
                        load_x(i, k + 2)
                    if not before:
                        for n in ((4,), (5,), (6, 7), ())[g]:
                            load_adapter(n)
                    if after:
                        wait_apart(sp, st_mm, UNITS * s + T * g + T)
                        copy_q(s + 1, g)
                    if g == 2 and ahead:
                        wait_apart(sp, mask_ready, s + 2)
                        load_mask(i, k + 2)
                    if before:
                        for t in ((), (0,), (1,), (2, 3))[g]:
                            wait_apart(sp, ffn_bank_read, 4 * s + t + 1)
                            sp.dma_start(chunk_of(out_v, i, k - 1)[:, t, :],
                                         xres[(k - 1) % 2][:, t, :]).then_inc(stored, 16)
                if before and after:
                    wait_apart(sp, stored, 64 * s)
                    load_res(i, k + 1)

            in_steps(sp, step)
            for t in range(T):
                sp.wait_ge(ffn_bank_read, 4 * LAST + 4 + t + 1)
                sp.dma_start(out_v[LAST % 2, LAST // 2][:, t, :], xres[AT_END][:, t, :]).then_inc(stored, 16)
            sp.wait_ge(stored, 64 * CHUNKS)

        @block.gpsimd
        def _(pool):
            def convert_mask(c, k):
                wait_apart(pool, mask_in, 16 * c + 16)
                nc.gpsimd.tensor_scalar(mask_bf[k % 2][:], mask_u8[:], MASKED, None,
                                        ALU.mult).then_inc(mask_ready, 1)

            def rstd_x(c):
                pool.wait_ge(stat1, 6 * c + 6)
                nc.gpsimd.tensor_tensor(rs1[:], ve1[:], m_half[:], ALU.pow).then_inc(rstd1, 1)

            def norm_x(c, t):
                wait_apart(pool, rstd1, c + 1)
                nc.gpsimd.tensor_scalar(xin[:, t, :], xin[:, t, :], nm1[:, t:t + 1],
                                        rs1[:, t:t + 1], ALU.add, ALU.mult).then_inc(xn_ready, 1)

            def divide(s, j):
                pool.wait_ge(inv_ready, UNITS * s + j + 1)
                nc.gpsimd.tensor_tensor(probs[j % 4][:, :, 0:M], probs[j % 4][:, :, 0:M],
                                        z_inv[:, j % 4, :].unsqueeze(2).to_broadcast([P, HG, M]),
                                        ALU.mult).then_inc(norm_ready, 1)

            def norm_h(f, t, at):
                pool.wait_ge(stat2, 3 * f + 3)
                nc.gpsimd.tensor_tensor(rs2[:, t:t + 1], ve2[:, t:t + 1], m_half[:, t:t + 1],
                                        ALU.pow).then_inc(rstd2, 1)
                wait_apart(pool, rstd2, f + 1)
                nc.gpsimd.tensor_scalar(x1n[t % 2][:], xres[at][:, t, :], nm2[:, t:t + 1],
                                        rs2[:, t:t + 1], ALU.add, ALU.mult).then_inc(h_ready, 1)

            def add_adapter_bias(f, t, at):
                pool.wait_ge(h_ready, f + 1)
                nc.gpsimd.tensor_tensor(xres[at][:, t, :], xres[at][:, t, :], bias_f[:],
                                        ALU.add).then_inc(x1b_ready, 1)

            nc.gpsimd.memset(m_half[:], -0.5).then_inc(setup_p, 1)
            pool.wait_ge(setup_p, 1)
            rstd_x(0)
            for t in range(T):
                norm_x(0, t)
            convert_mask(0, 0)
            rstd_x(1)
            for t in range(T):
                norm_x(1, t)
            divide(0, 0)

            def step(i, k, before=True, after=True, ahead=True):
                s = 2 * i + k

                def add_bias(t):
                    pool.wait_ge(res_in[k % 2], 16 * (i + k // 2) + 16)
                    if not before:
                        pool.wait_ge(setup_v, 2)
                    nc.gpsimd.tensor_tensor(xres[k % 2][:, t, :], xres[k % 2][:, t, :], bias_p[:],
                                            ALU.add).then_inc(res_ready, 1)

                for g in range(KB):
                    for p in range(T):
                        j = T * g + p
                        if in_range(j + 1, before, after):
                            divide(s, j + 1)
                        if p == 0 and g >= 1:
                            add_bias(g - 1)
                        if (g, p) == (1, 2) and after:
                            if before:
                                pool.wait_ge(st_read, UNITS * s)
                            convert_mask(s + 1, k + 1)
                        if p == 2 and before:
                            norm_h(4 * s - 4 + g, g, (k - 1) % 2)
                        if p == 3 and before:
                            add_adapter_bias(4 * s - 4 + g, g, (k - 1) % 2)
                        if g == 3 and ahead:
                            if p == 0:
                                rstd_x(s + 2)
                            norm_x(s + 2, p)
                add_bias(T - 1)
                if not before:
                    pool.wait_ge(s_wmix, 2 * NK)

            in_steps(pool, step)
            for t in range(T):
                if t >= 2:
                    pool.wait_ge(ht_mm, 4 * LAST + t - 1)
                norm_h(4 * LAST + t, t, AT_END)
                add_adapter_bias(4 * LAST + t, t, AT_END)

        @block.scalar
        def _(act):
            def xt_high(c, banks, tiles=range(T)):
                for t in tiles:
                    act.wait_ge(xt_mm, 4 * c + t + 1)
                    nc.scalar.copy(xn_hi[:, :, t * P:t * P + P],
                                   bank[banks[t]][:].rearrange("p (k n) -> p k n", k=KB)).then_inc(xt_hi, 1)

            def q_high(c, g, src):
                act.wait_ge(q_mm, 4 * c + g + 1)
                if g >= 2:
                    act.wait_ge(q_in[g - 2], REP * c + REP)
                elif not (isinstance(c, int) and c == 0):
                    act.wait_ge(q_in[g + 2], REP * c)
                nc.scalar.copy(q_hi[g % 2][:], bank[src][:]).then_inc(qh_ready, 1)

            def exponentials(s, j, first):
                act.wait_ge(st_read, UNITS * s + j + 1)
                if not (first and j < 4):
                    act.wait_ge(pt_mm, UNITS * s + j - 3)
                for h in range(HG):
                    last = nc.scalar.activation(probs[j % 4][:, h, :], scores[j % 2][:, h, :], ACT.Exp,
                                                bias=neg_max[:, j % 4, h:h + 1], scale=-1.0,
                                                accum_out=z_sum[:, j % 4, h:h + 1])
                last.then_inc(exp_ready, 1)

            def o_high(n, g, at):
                act.wait_ge(u_mm, T * n + T)
                nc.scalar.copy(o_hi[at][:, g, :], bank[O_BANK][:]).then_inc(oh_ready, 1)

            def h_high(f, t, src):
                act.wait_ge(ht_mm, f + 1)
                nc.scalar.copy(h_hi[t % 2][:], bank[src][:].rearrange("p (k n) -> p k n", k=KB)).then_inc(ht_hi, 1)

            for b in range(B):
                act.wait_ge(s_ctxt_mm, b + 1)
                nc.scalar.copy(ctx_t[:, :, b * M:b * M + M],
                               bank[4 + b][:].rearrange("p (k n) -> p k n", k=KB)).then_inc(s_ctxt, 1)
            xt_high(0, range(T))
            act.wait_ge(s_wq, 16)
            nc.scalar.copy(by_channel(wq_hi[:]), wq_raw[:].rearrange("p k (g h d) -> p (k g) h d", h=HG, d=D)).then_inc(s_wqs, 1)
            act.wait_ge(s_gates, 64)
            nc.scalar.activation(tanh_g[:], gates[:], ACT.Tanh).then_inc(s_tanh, 1)
            act.wait_ge(setup_v, 3)
            nc.scalar.copy(wp_hi[:], wp_raw[:]).then_inc(s_wph, 1)
            for g in range(KB):
                act.wait_ge(s_k_mm, g + 1)
                nc.scalar.copy(k_hi[:].rearrange("p (b g) m -> p g b m", b=B)[:, g],
                               bank[g][:, 0:B * M].rearrange("p (b m) -> p b m", b=B)).then_inc(s_khi, 1)
            for g in range(KB):
                q_high(0, g, g)
            exponentials(0, 0, True)
            exponentials(0, 1, True)
            for b in range(B):
                act.wait_ge(s_v_mm, b + 1)
                nc.scalar.copy(v_sb[:, b, :], bank[6 + b][:]).then_inc(s_v, 1)

            def step(i, k, before=True, after=True, ahead=True):
                s = 2 * i + k

                def move_probs(j):
                    act.wait_ge(pt_mm, UNITS * s + j + 1)
                    if before or j >= 2:
                        act.wait_ge(u_mm, UNITS * s + j - 1)
                    nc.scalar.copy(probs_t[j % 2][:].rearrange("p h n -> p (h n)"),
                                   bank[PT_BANK[j % 2]][:]).then_inc(pt_ready, 1)

                for g in range(KB):
                    for p in range(T):
                        j = T * g + p
                        if j == 0 and before:
                            o_high(KB * s - 1, KB - 1, (k - 1) % 2)
                        if j == 0 and after:
                            xt_high(s + 1, XT_BANKS, (0, 1))
                        if j == UNITS - 1 and before:
                            move_probs(j)
                            h_high(4 * s - 4 + g, g, FFN_BANK)
                        if in_range(j + 2, before, after):
                            exponentials(s, j + 2, not before)
                        if j < UNITS - 1 or not before:
                            move_probs(j)
                        if p == 0 and g >= 1:
                            o_high(KB * s + g - 1, g - 1, k % 2)
                        if j == 0 and after:
                            xt_high(s + 1, XT_BANKS, (2, 3))
                        if p == 3 and before and g < 3:
                            h_high(4 * s - 4 + g, g, FFN_BANK)
                        if p == 3 and after:
                            q_high(s + 1, g, Q_BANK)
                        if not before and g == 3:
                            act.wait_ge(s_wft_mm, p + 1)
                            nc.scalar.copy(wf_hi[:, p, :], bank[WF_BANKS[p]][:]).then_inc(s_wf, 1)

            in_steps(act, step)
            o_high(KB * LAST + KB - 1, KB - 1, AT_END)
            for t in range(T):
                h_high(4 * LAST + t, t, LAST_FFN_BANKS[t])

        @block.vector
        def _(dve):
            def stats_x(c, t):
                dve.wait_ge(x_in, 16 * c + 16)
                nc.vector.bn_stats(bn1[:, t, :], xin[:, t, :]).then_inc(stat1, 1)
                if t == T - 1:
                    wait_apart(dve, stat1, 6 * c + 4)
                    for u in range(T):
                        last = nc.vector.bn_aggr(mv1[:, u, :], bn1[:, u, :])
                    last.then_inc(stat1, 1)
                    dve.wait_ge(stat1, 6 * c + 5)
                    nc.vector.tensor_scalar(nm1[:], mv1[:, :, 0], -1.0, None, ALU.mult)
                    nc.vector.tensor_scalar(ve1[:], mv1[:, :, 1], EPS, None, ALU.add).then_inc(stat1, 1)

            def xt_low(c, banks, tiles=range(T)):
                for t in tiles:
                    dve.wait_ge(xt_hi, 4 * c + t + 1)
                    part = slice(t * P, t * P + P)
                    nc.vector.tensor_tensor(xn_lo[:, :, part], bank[banks[t]][:].rearrange("p (k n) -> p k n", k=KB),
                                            xn_hi[:, :, part].bitcast(F32), ALU.subtract).then_inc(xt_lo, 1)

            def q_low(c, g, src):
                dve.wait_ge(qh_ready, 4 * c + g + 1)
                nc.vector.tensor_tensor(q_lo[g % 2][:], bank[src][:], q_hi[g % 2][:].bitcast(F32),
                                        ALU.subtract).then_inc(ql_ready, 1)

            def mask_scores(s, k, j, first):
                c = j // UNITS
                wait_apart(dve, mask_ready, s + c + 1)
                wait_apart(dve, st_mm, UNITS * s + j + 1)
                if not (first and j < 2):
                    wait_apart(dve, exp_ready, UNITS * s + j - 1)
                for h in range(HG):
                    last = nc.vector.tensor_tensor_reduce(
                        out=scores[j % 2][:, h, 0:M], in0=bank[S_BANK[j % 2]][:, h * M:h * M + M],
                        in1=mask_bf[(k + c) % 2][:, j % T, :], scale=-SCALE, scalar=0.0,
                        op0=ALU.add, op1=ALU.min, accum_out=neg_max[:, j % 4, h:h + 1])
                last.then_inc(st_read, 1)

            def invert(s, j):
                dve.wait_ge(exp_ready, UNITS * s + j + 1)
                nc.vector.reciprocal(z_inv[:, j % 4, :], z_sum[:, j % 4, :]).then_inc(inv_ready, 1)

            def mix_adapter(k):
                dve.wait_ge(s_w[k % 2], 32 * (k // 2) + 32)
                if k == 0:
                    dve.wait_ge(setup_v, 1)
                    nc.vector.tensor_scalar(w_acc[:], w_raw[0][:], mix[:, 0:1], None, ALU.mult).then_inc(s_wmix, 1)
                    nc.vector.tensor_scalar(bias_f[:], b_raw[0][:], mix[:, 0:1], None, ALU.mult).then_inc(s_wmix, 1)
                    return
                dve.wait_ge(s_wmix, 2 * k)
                flat = lambda a: a[:].rearrange("p k n -> p (k n)")
                nc.vector.scalar_tensor_tensor(out=flat(w_acc), in0=flat(w_raw[k % 2]), scalar=mix[:, k:k + 1],
                                               in1=flat(w_acc), op0=ALU.mult, op1=ALU.add).then_inc(s_wmix, 1)
                nc.vector.scalar_tensor_tensor(out=bias_f[:], in0=b_raw[k % 2][:], scalar=mix[:, k:k + 1],
                                               in1=bias_f[:], op0=ALU.mult, op1=ALU.add).then_inc(s_wmix, 1)

            def o_low(n, g, at):
                dve.wait_ge(oh_ready, n + 1)
                nc.vector.tensor_tensor(o_lo[at][:, g, :], bank[O_BANK][:], o_hi[at][:, g, :].bitcast(F32),
                                        ALU.subtract).then_inc(ol_ready, 1)

            def add_x1(f, t, at, src):
                xr = xres[at][:, t, :]
                dve.wait_ge(pj_mm, f + 1)
                dve.wait_ge(res_ready, f + 1)
                nc.vector.tensor_tensor(xr, bank[src][:], xr, ALU.add).then_inc(x1_ready, 1)
                dve.wait_ge(x1_ready, f + 1)
                nc.vector.bn_stats(bn2[:, t, :], xr).then_inc(stat2, 1)
                wait_apart(dve, stat2, 3 * f + 1)
                nc.vector.bn_aggr(mv2[:, t, :], bn2[:, t, :]).then_inc(stat2, 1)
                dve.wait_ge(stat2, 3 * f + 2)
                nc.vector.tensor_scalar(nm2[:, t:t + 1], mv2[:, t, 0:1], -1.0, None, ALU.mult)
                nc.vector.tensor_scalar(ve2[:, t:t + 1], mv2[:, t, 1:2], EPS, None, ALU.add).then_inc(stat2, 1)

            def h_low(f, t, src):
                dve.wait_ge(ht_hi, f + 1)
                nc.vector.tensor_tensor(h_lo[t % 2][:], bank[src][:].rearrange("p (k n) -> p k n", k=KB),
                                        h_hi[t % 2][:].bitcast(F32), ALU.subtract).then_inc(ht_lo, 1)

            def add_output(f, t, at, src):
                dve.wait_ge(ff_mm, f + 1)
                dve.wait_ge(x1b_ready, f + 1)
                nc.vector.tensor_tensor(xres[at][:, t, :], bank[src][:], xres[at][:, t, :],
                                        ALU.add).then_inc(ffn_bank_read, 1)

            for i in range(2):
                nc.vector.memset(scores[i][:, :, M:M + 1], 0.0)
            for t in range(T):
                stats_x(0, t)
            dve.wait_ge(s_wkv, 16)
            for k in range(KB):
                last = nc.vector.tensor_copy(wk_sb[:, k, :].rearrange("p (g d h) -> p g h d", h=HG, d=D),
                                             wkv_raw[:, k, 0:C].rearrange("p (g h d) -> p g h d", h=HG, d=D))
            last.then_inc(s_wk, 1)
            xt_low(0, range(T))
            dve.wait_ge(s_wqs, 1)
            nc.vector.tensor_tensor(by_channel(wq_lo[:]), wq_raw[:].rearrange("p k (g h d) -> p (k g) h d", h=HG, d=D),
                                    by_channel(wq_hi[:].bitcast(F32)), ALU.subtract).then_inc(s_wqs, 1)
            dve.wait_ge(s_tanh, 1)
            nc.vector.tensor_scalar(mix[:], mix[:], tanh_g[:, 1:2], None, ALU.mult).then_inc(setup_v, 1)
            nc.vector.tensor_scalar(bias_p[:], bias_p[:], tanh_g[:, 0:1], None, ALU.mult).then_inc(setup_v, 1)
            dve.wait_ge(s_wp, 16)
            nc.vector.tensor_scalar(wp_raw[:], wp_raw[:], tanh_g[:, 0:1], None, ALU.mult).then_inc(setup_v, 1)
            for g in range(KB):
                dve.wait_ge(s_khi, g + 1)
                nc.vector.tensor_tensor(k_lo[:].rearrange("p (b g) m -> p g b m", b=B)[:, g],
                                        bank[g][:, 0:B * M].rearrange("p (b m) -> p b m", b=B),
                                        k_hi[:].bitcast(F32).rearrange("p (b g) m -> p g b m", b=B)[:, g],
                                        ALU.subtract).then_inc(s_klo, 1)
            dve.wait_ge(s_wph, 1)
            nc.vector.tensor_tensor(wp_lo[:], wp_raw[:], wp_hi[:].bitcast(F32), ALU.subtract).then_inc(s_wpl, 1)
            q_low(0, 0, 0)
            for t in range(T):
                stats_x(1, t)
            q_low(0, 1, 1)
            mix_adapter(0)
            q_low(0, 2, 2)
            q_low(0, 3, 3)
            mask_scores(0, 0, 0, True)
            mask_scores(0, 0, 1, True)
            mix_adapter(1)
            invert(0, 0)
            mask_scores(0, 0, 2, True)
            invert(0, 1)

            def step(i, k, before=True, after=True, ahead=True):
                s = 2 * i + k

                for g in range(KB):
                    f, at = 4 * s - 4, (k - 1) % 2
                    for p in range(T):
                        j = T * g + p
                        if p == 0 and in_range(j - 1, before, after):
                            o_low(KB * s + g - 1, (g - 1) % KB, (k + (g - 1) // KB) % 2)
                        if j == 0 and after:
                            xt_low(s + 1, XT_BANKS, (0, 1))
                        if in_range(j + 3, before, after):
                            mask_scores(s, k, j + 3, not before)
                        if j == 0 and after:
                            xt_low(s + 1, XT_BANKS, (2, 3))
                        if p == 1 and before:
                            add_x1(f + g, g, at, PROJ_BANK)
                        if g == 2 and ahead:
                            stats_x(s + 2, p)
                        if j == UNITS - 1 and before:
                            h_low(f + g, g, FFN_BANK)
                        if in_range(j + 2, before, after):
                            invert(s, j + 2)
                        if not before and p % 2 == 1 and g < 3:
                            mix_adapter(2 + 2 * g + p // 2)
                        if not before and g == 3:
                            dve.wait_ge(s_wf, p + 1)
                            nc.vector.tensor_tensor(wf_lo[:, p, :], bank[WF_BANKS[p]][:], wf_hi[:, p, :].bitcast(F32),
                                                    ALU.subtract).then_inc(ffn_bank_read, 1)
                        if p == 2 and before and g >= 1:
                            add_output(f + g - 1, g - 1, at, FFN_BANK)
                        if p == 3 and before and g < 3:
                            h_low(f + g, g, FFN_BANK)
                        if p == 3 and after:
                            q_low(s + 1, g, Q_BANK)
                if before:
                    add_output(f + T - 1, T - 1, at, FFN_BANK)

            in_steps(dve, step)
            f = 4 * LAST
            o_low(KB * LAST + KB - 1, KB - 1, AT_END)
            for t in range(T):
                if t == 3:
                    h_low(f, 0, LAST_FFN_BANKS[0])
                add_x1(f + t, t, AT_END, LAST_PROJ_BANKS[t])
            h_low(f + 1, 1, LAST_FFN_BANKS[1])
            for t in range(2, T):
                add_output(f + t - 2, t - 2, AT_END, LAST_FFN_BANKS[t - 2])
                h_low(f + t, t, LAST_FFN_BANKS[t])
            for t in range(2, T):
                add_output(f + t, t, AT_END, LAST_FFN_BANKS[t])

        @block.tensor
        def _(pe):
            mm = nc.tensor.matmul

            def split_product(dst, lhs_h, lhs_l, rhs_h, rhs_l, blocks=range(KB)):
                for k in blocks:
                    mm(dst, lhs_h(k), rhs_h(k), start=(k == 0), stop=False)
                    mm(dst, lhs_h(k), rhs_l(k), start=False, stop=False)
                    last = mm(dst, lhs_l(k), rhs_h(k), start=False, stop=(k == KB - 1))
                return last

            def transpose_x(c, t, dst):
                pe.wait_ge(xn_ready, 4 * c + t + 1)
                for k in range(KB):
                    last = nc.tensor.transpose(bank[dst][:, k * P:k * P + P], xin[:, t, k * P:k * P + P], ident)
                last.then_inc(xt_mm, 1)

            def queries(g, dst, blocks=range(KB)):
                cols = slice(g * P, g * P + P)
                return split_product(bank[dst][:], lambda k: wq_hi[:, k, cols], lambda k: wq_lo[:, k, cols],
                                     lambda k: xn_hi[:, k, :], lambda k: xn_lo[:, k, :], blocks)

            def unit_scores(s, k, j, first):
                c, g, t = j // UNITS, j % UNITS // T, j % T
                if t == 0:
                    pe.wait_ge(q_in[g], REP * (s + c) + REP)
                if not (first and j < 2):
                    pe.wait_ge(st_read, UNITS * s + j - 1)
                for h in range(HG):
                    last = mm(bank[S_BANK[j % 2]][:, h * M:h * M + M],
                              q_stack[0:KROWS, HG * g + h, t * P:t * P + P],
                              k_stack[0:KROWS, h, (k + c) % 2 * KB + g, :], start=True, stop=True)
                last.then_inc(st_mm, 1)

            def products(units, groups, k, j, first):
                c, g, t = j // UNITS, j % UNITS // T, j % T
                pe.wait_ge(pt_ready, units + j + 1)
                if t == 0 and not first:
                    pe.wait_ge(ol_ready, groups + j // T)
                for h in range(HG):
                    at = D * (HG * g + h)
                    last = mm(bank[O_BANK][D * h:D * h + D, t * P:t * P + P],
                              v_sb[:, (k + c) % 2, at:at + D], probs_t[j % 2][:, h, :],
                              start=True, stop=True, skip_group_check=True)
                last.then_inc(u_mm, 1)

            def project(at, t, dst, blocks=range(KB)):
                part = slice(t * P, t * P + P)
                return split_product(bank[dst][:], lambda q: o_hi[at][:, q, part], lambda q: o_lo[at][:, q, part],
                                     lambda q: wp_hi[:, q, :], lambda q: wp_lo[:, q, :], blocks)

            def transpose_h(f, t, dst):
                pe.wait_ge(h_ready, f + 1)
                for q in range(KB):
                    last = nc.tensor.transpose(bank[dst][:, q * P:q * P + P], x1n[t % 2][:, q * P:q * P + P], ident)
                last.then_inc(ht_mm, 1)

            def adapt(f, t, dst):
                pe.wait_ge(ht_lo, f + 1)
                split_product(bank[dst][:], lambda q: h_hi[t % 2][:, q, :], lambda q: h_lo[t % 2][:, q, :],
                              lambda q: wf_hi[:, q, :], lambda q: wf_lo[:, q, :]).then_inc(ff_mm, 1)

            pe.wait_ge(s_ident, 16)
            pe.wait_ge(s_ctx, 16)
            for b in range(B):
                for k in range(KB):
                    last = nc.tensor.transpose(bank[4 + b][:, k * P:k * P + P], ctx_sb[:, b, k * P:k * P + P], ident)
                last.then_inc(s_ctxt_mm, 1)
            for t in range(T):
                transpose_x(0, t, t)
            pe.wait_ge(s_wkv, 16)
            pe.wait_ge(s_ctxt, B)
            pe.wait_ge(s_wk, 1)
            for g in range(KB):
                pe.wait_ge(xt_lo, g + 1)
                for k in range(KB):
                    last = mm(bank[g][:, 0:B * M],
                              wk_sb[:, k, g * P:g * P + P], ctx_t[:, k, :],
                              start=(k == 0), stop=(k == KB - 1))
                last.then_inc(s_k_mm, 1)
            pe.wait_ge(s_wqs, 2)
            for g in range(KB):
                pe.wait_ge(s_klo, g + 1)
                queries(g, g).then_inc(q_mm, 1)
            pe.wait_ge(s_kst, 16 * 3)
            pe.wait_ge(ql_ready, 2)
            for j in range(3):
                unit_scores(0, 0, j, True)
            for b in range(B):
                for k in range(KB):
                    last = mm(bank[6 + b][:], ctx_t[:, k, b * M:b * M + M], wkv_raw[:, k, C:2 * C],
                              start=(k == 0), stop=(k == KB - 1))
                last.then_inc(s_v_mm, 1)
            pe.wait_ge(ql_ready, 4)
            pe.wait_ge(s_v, B)

            def step(i, k, before=True, after=True, ahead=True):
                s = 2 * i + k

                def transpose_probs(j):
                    pe.wait_ge(norm_ready, UNITS * s + j + 1)
                    if before or j >= 2:
                        pe.wait_ge(pt_ready, UNITS * s + j - 1)
                    for h in range(HG):
                        last = nc.tensor.transpose(bank[PT_BANK[j % 2]][:, h * P:h * P + P],
                                                   probs[j % 4][:, h, 0:M], ident)
                    last.then_inc(pt_mm, 1)

                for g in range(KB):
                    f = 4 * s - 4 + g
                    for p in range(T):
                        j = T * g + p
                        if j == 0 and before:
                            products(UNITS * s, KB * s, k, -1, False)
                        if in_range(j + 3, before, after):
                            unit_scores(s, k, j + 3, not before)
                        transpose_probs(j)
                        if j >= 1:
                            products(UNITS * s, KB * s, k, j - 1, not before and j == 1)
                        if j == 0:
                            if after:
                                if before:
                                    pe.wait_ge(ffn_bank_read, 4 * s)
                                pe.wait_ge(ql_ready, 4 * s + 4)
                                transpose_x(s + 1, 0, XT_BANKS[0])
                                transpose_x(s + 1, 1, XT_BANKS[1])
                            if before:
                                pe.wait_ge(ol_ready, KB * s)
                                pe.wait_ge(s_wpl, 1)
                                project((k - 1) % 2, g, PROJ_BANK, range(KB // 2))
                            if after:
                                for t in (2, 3):
                                    pe.wait_ge(xt_lo, 4 * s + 4 + t - 1)
                                    transpose_x(s + 1, t, XT_BANKS[t])
                            if before:
                                project((k - 1) % 2, g, PROJ_BANK, range(KB // 2, KB)).then_inc(pj_mm, 1)
                        elif p == 0 and before:
                            pe.wait_ge(x1_ready, f)
                            project((k - 1) % 2, g, PROJ_BANK).then_inc(pj_mm, 1)
                        if g == 0 and p in (1, 2) and after:
                            if p == 1:
                                pe.wait_ge(xt_lo, 4 * s + 8)
                                queries(g, Q_BANK, range(KB // 2))
                            else:
                                queries(g, Q_BANK, range(KB // 2, KB)).then_inc(q_mm, 1)
                        if g >= 1 and p == 1 and before:
                            adapt(f - 1, g - 1, FFN_BANK)
                        if g >= 1 and p == 2 and after:
                            pe.wait_ge(ql_ready, 4 * s + 4 + g)
                            queries(g, Q_BANK, range(KB - 1))
                        if p == 3 and before:
                            pe.wait_ge(ffn_bank_read, 4 * s + g)
                            transpose_h(f, g, FFN_BANK)
                        if g >= 1 and p == 3 and after:
                            queries(g, Q_BANK, range(KB - 1, KB)).then_inc(q_mm, 1)
                        if g == T - 1 and p == 3 and before:
                            adapt(f, g, FFN_BANK)
                        if not before and g == 3:
                            if p == 0:
                                pe.wait_ge(s_wmix, 2 * NK)
                            if p >= 2:
                                pe.wait_ge(ffn_bank_read, p - 1)
                            for o in range(KB):
                                last = nc.tensor.transpose(bank[WF_BANKS[p]][:, o * P:o * P + P],
                                                           w_acc[:, o, p * P:p * P + P], ident)
                            last.then_inc(s_wft_mm, 1)

            in_steps(pe, step)
            products(UNITS * LAST, KB * LAST, LAST, UNITS - 1, False)
            f, ffn_bank = 4 * LAST, LAST_FFN_BANKS
            pe.wait_ge(ol_ready, KB * CHUNKS)
            for t in range(3):
                project(AT_END, t, LAST_PROJ_BANKS[t]).then_inc(pj_mm, 1)
            transpose_h(f, 0, ffn_bank[0])
            project(AT_END, 3, LAST_PROJ_BANKS[3]).then_inc(pj_mm, 1)
            transpose_h(f + 1, 1, ffn_bank[1])
            for t in range(2, T):
                adapt(f + t - 2, t - 2, ffn_bank[t - 2])
                transpose_h(f + t, t, ffn_bank[t])
            for t in range(2, T):
                adapt(f + t, t, ffn_bank[t])


_INS = ['x', 'ctx_1024', 'mask_BxSxS2_bk0', 'g_xattn', 'g_ffn', 'L0_xattn_Wq', 'L0_xattn_Wkv',
        'L0_xattn_Wproj', 'L0_xattn_bproj', 'L0_ffn_W', 'L0_ffn_b', 'L0_ffn_ids', 'L0_ffn_weights']


def kernel(**inputs):
    import concourse.bacc as bacc
    from concourse.bass_utils import run_bass_kernel_spmd

    nc = bacc.Bacc("TRN2", target_bir_lowering=False, num_devices=1, dynamic_dma_scratch_size=64)
    arrays, args = {}, []

    def add(name, a):
        arrays[name] = a
        args.append(nc.dram_tensor(name, a.shape, mybir.dt.from_np(a.dtype), kind="ExternalInput").ap())

    for name in _INS:
        a = np.ascontiguousarray(inputs[name])
        add(f"in_{name}", a)
    add("const_f32", np.eye(128, dtype=np.float32))
    shape = inputs['x'].shape
    args.append(nc.dram_tensor("out_0", shape, mybir.dt.float32, kind="ExternalOutput").ap())
    flamingo_program(nc, *args)
    r = run_bass_kernel_spmd(nc, [arrays], core_ids=[0])
    return r.results[0]["out_0"]
```

```python
from contextlib import ExitStack

import numpy as np

import concourse.bass as bass
from concourse import mybir


def flamingo_program(nc, x, ctx_in, mask, g_attn, g_ffn, wq, wkv, wproj, bproj, ffn_w, ffn_b, ids,
                     weights, eye, out):
    F32, F32R, BF16, U8 = mybir.dt.float32, mybir.dt.float32r, mybir.dt.bfloat16, mybir.dt.uint8
    ALU, ACT = mybir.AluOpType, mybir.ActivationFunctionType

    P = 128
    B, N, C = x.shape
    M = ctx_in.shape[1]
    H = 16
    D = C // H
    SCALE = float(D) ** -0.5
    MASKED = -1e38
    EPS = 1e-5
    KB = C // P
    HG = P // D
    T = 4
    TOK = T * P
    CHUNKS = B * N // TOK
    UNITS = KB * T
    LAST, AT_END = CHUNKS - 1, (CHUNKS - 1) % 2
    KROWS = 3 * D
    NK = ids.shape[0]
    REP = 16 * 3
    assert NK == 2 * KB
    assert M == P and HG == 4 and KB == 4 and B == 2 and CHUNKS % 2 == 0

    x_v = x.rearrange("b (c t p) d -> b c p t d", t=T, p=P)
    out_v = out.rearrange("b (c t p) d -> b c p t d", t=T, p=P)
    mask_v = mask.rearrange("b (c t p) m -> b c p t m", t=T, p=P)
    ffn_v = ffn_w.rearrange("a (t p) d -> a p t d", p=P)

    ctx = ExitStack()
    with ctx:
        def sb(name, shape, dt, where=ctx):
            return where.enter_context(nc.sbuf_tensor(name, shape, dt))

        def sem(name):
            return ctx.enter_context(nc.semaphore(name))

        with ExitStack() as early:
            wq_raw = sb("wq_raw", [P, KB, C], F32, early)
        q_stack = sb("q_stack", [P, H, TOK], F32R)
        with ExitStack() as early:
            wkv_raw = sb("wkv_raw", [P, KB, 2 * C], F32, early)
        o_hi, o_lo = [None, None], [None, None]
        o_hi[0] = sb("o_hi0", [P, KB, TOK], F32R)
        o_lo[0] = sb("o_lo0", [P, KB, TOK], F32R)
        with ExitStack() as early:
            w_raw = [sb(f"w_raw{i}", [P, KB, C], F32, early) for i in range(2)]
        o_hi[1] = sb("o_hi1", [P, KB, TOK], F32R)
        o_lo[1] = sb("o_lo1", [P, KB, TOK], F32R)
        with ExitStack() as early:
            w_acc = sb("w_acc", [P, KB, C], F32, early)
        h_hi = [sb(f"h_hi{i}", [P, KB, P], F32R) for i in range(2)]
        h_lo = [sb(f"h_lo{i}", [P, KB, P], F32R) for i in range(2)]
        with ExitStack() as early:
            ctx_sb = sb("ctx_sb", [P, B, C], F32, early)
            ctx_t = sb("ctx_t", [P, KB, B * M], F32, early)
            wp_raw = sb("wp_raw", [P, KB, C], F32, early)
        xres = [sb(f"xres{i}", [P, T, C], F32) for i in range(2)]
        xn_hi = sb("xn_hi", [P, KB, TOK], F32R)
        xn_lo = sb("xn_lo", [P, KB, TOK], F32R)
        xin = sb("xin", [P, T, C], F32)
        with ExitStack() as early:
            b_rows = sb("b_rows", [NK, C], F32, early)
        x1n = [sb(f"x1n{i}", [P, C], F32) for i in range(2)]
        wq_hi = sb("wq_hi", [P, KB, C], F32R)
        wq_lo = sb("wq_lo", [P, KB, C], F32R)
        wp_hi = sb("wp_hi", [P, KB, C], F32R)
        wp_lo = sb("wp_lo", [P, KB, C], F32R)
        with ExitStack() as early:
            wk_sb = sb("wk_sb", [P, KB, C], F32, early)
        wf_hi = sb("wf_hi", [P, KB, C], F32R)
        wf_lo = sb("wf_lo", [P, KB, C], F32R)
        k_stack = sb("k_stack", [P, HG, B * KB, M], F32R)
        v_sb = sb("v_sb", [P, B, C], F32)
        bias_p = sb("bias_p", [P, C], F32)
        bias_f = sb("bias_f", [P, C], F32)
        with ExitStack() as early:
            k_hi = sb("k_hi", [P, B * KB, M], F32R, early)
            k_lo = sb("k_lo", [P, B * KB, M], F32R, early)
        probs = [sb(f"probs{i}", [P, HG, M + 1], F32) for i in range(4)]
        q_hi = [sb(f"q_hi{i}", [P, TOK], F32R) for i in range(2)]
        q_lo = [sb(f"q_lo{i}", [P, TOK], F32R) for i in range(2)]
        scores = [sb(f"scores{i}", [P, HG, M + 1], F32) for i in range(2)]
        probs_t = [sb(f"probs_t{i}", [P, HG, 2 * P], F32) for i in range(2)]
        neg_max = sb("neg_max", [P, 4, HG], F32)
        z_sum = sb("z_sum", [P, 4, HG], F32)
        z_inv = sb("z_inv", [P, 4, HG], F32)
        ident_sb = sb("ident_sb", [P, P], F32)
        ident = ident_sb[:]
        mask_u8 = sb("mask_u8", [P, T, M], U8)
        mask_bf = [sb(f"mask_bf{i}", [P, T, M], BF16) for i in range(2)]
        gates = sb("gates", [P, 2], F32)
        tanh_g = sb("tanh_g", [P, 2], F32)
        mix = sb("mix", [P, NK], F32)
        mix_rows = sb("mix_rows", [NK, 1], F32)
        mix_cols = sb("mix_cols", [NK, P], F32)
        bn1 = sb("bn1", [P, T, 6], F32)
        mv1 = sb("mv1", [P, T, 2], F32)
        nm1 = sb("nm1", [P, T], F32)
        ve1 = sb("ve1", [P, T], F32)
        rs1 = sb("rs1", [P, T], F32)
        bn2 = sb("bn2", [P, T, 6], F32)
        mv2 = sb("mv2", [P, T, 2], F32)
        nm2 = sb("nm2", [P, T], F32)
        ve2 = sb("ve2", [P, T], F32)
        rs2 = sb("rs2", [P, T], F32)
        m_half = sb("m_half", [P, T], F32)

        bank = [ctx.enter_context(nc.psum_tensor(f"bank{i}", [P, TOK], F32)) for i in range(8)]
        S_BANK, PT_BANK, O_BANK = (0, 1), (2, 3), 4
        PROJ_BANK, Q_BANK, FFN_BANK = 5, 6, 7
        LAST_PROJ_BANKS, LAST_FFN_BANKS = (5, 0, 1, 2), (7, 6, 3, 4)
        XT_BANKS = (6, 7, 6, 7)
        Q_BLOCKS = (((), (0, 1), (2,), (3,)),) + (((), (), (0, 1, 2), (3,)),) * 2 + (((), (), (0,), (1, 2, 3)),)
        K_BANKS = (4, 5, 6, 7)
        V_BANKS = (6, 5)
        BIAS_BANK = 7
        WF_BANKS = (5, 7, 5, 7)

        s_ident, s_gates, s_ctx = sem("ident_in"), sem("gates_in"), sem("ctx_in")
        s_wkv, s_wv, s_wq, s_wp = sem("wk_in"), sem("wv_in"), sem("wq_in"), sem("wp_in")
        s_wk = sem("wk_ready")
        s_w, s_wmix = [sem("w_in0"), sem("w_in1")], sem("w_mixed")
        s_b, s_b_mm, s_bf = sem("b_in"), sem("b_mm"), sem("bias_f_ready")
        x_in, mask_in = sem("x_in"), sem("mask_in")
        res_in = [sem("res_in0"), sem("res_in1")]
        setup_v, setup_p = sem("setup_v"), sem("setup_p")
        s_tanh, s_ctxt_mm, s_ctxt = sem("tanh_ready"), sem("ctx_t_mm"), sem("ctx_t_ready")
        s_k_mm, s_v_mm, s_v = sem("k_mm"), sem("v_mm"), sem("v_ready")
        s_khi, s_klo, s_kst = sem("k_hi_ready"), sem("k_lo_ready"), sem("k_stack_in")
        s_wqs, s_wph, s_wpl = sem("wq_split"), sem("wp_hi_ready"), sem("wp_lo_ready")
        s_wft_mm, s_wf = sem("wf_t_mm"), sem("wf_hi_ready")
        stat1, rstd1, xn_ready = sem("stat1"), sem("rstd1"), sem("xn_ready")
        xt_mm, xt_hi, xt_lo = sem("xt_mm"), sem("xt_hi"), sem("xt_lo")
        q_mm, qh_ready, ql_ready = sem("q_mm"), sem("qh_ready"), sem("ql_ready")
        q_in = [sem(f"q_in{g}") for g in range(KB)]
        mask_ready = sem("mask_ready")
        st_mm, st_read, exp_ready = sem("st_mm"), sem("st_read"), sem("exp_ready")
        inv_ready, norm_ready = sem("inv_ready"), sem("norm_ready")
        pt_mm, pt_ready = sem("pt_mm"), sem("pt_ready")
        u_mm = sem("u_mm")
        oh_ready, ol_ready = sem("oh_ready"), sem("ol_ready")
        res_ready = sem("res_ready")
        pj_mm, x1_ready, stat2 = sem("pj_mm"), sem("x1_ready"), sem("stat2")
        rstd2, h_ready, x1b_ready = sem("rstd2"), sem("h_ready"), sem("x1b_ready")
        ht_mm, ht_hi, ht_lo = sem("ht_mm"), sem("ht_hi"), sem("ht_lo")
        ff_mm, ffn_bank_read = sem("ff_mm"), sem("ffn_bank_read")
        stored = sem("stored")
        passed = sem("passed")

        block = ctx.enter_context(nc.Block())

        def wait_apart(engine, signal, value):
            engine.wait_ge(signal, value)
            engine.sem_inc(passed)

        def by_channel(a):
            return a.rearrange("p k (g d h) -> p (k g) h d", h=HG, d=D)

        def by_head(a):
            return a.rearrange("p k (g h d) -> p (k g) h d", h=HG, d=D)

        def in_steps(engine, step):
            loops = (CHUNKS - 4) // 2
            step(0, 0, before=False)
            with engine.Fori(0, loops) as i:
                step(i, 1)
                step(i, 2)
            step(loops, 1)
            step(loops, 2, ahead=False)
            step(loops + 1, 1, after=False, ahead=False)

        def in_range(j, before, after):
            return before if j < 0 else j < UNITS or after

        def chunk_of(view, i, k):
            c = i + k // 2
            if isinstance(c, int):
                return view[k % 2, c]
            return view[k % 2, bass.ds(c, 1)].rearrange("o p t d -> (o p) t d")

        @block.sync
        def _(sp):
            def load_x(i, k):
                sp.dma_start(xin[:], chunk_of(x_v, i, k)).then_inc(x_in, 16)

            def load_mask(i, k):
                sp.dma_start(mask_u8[:], chunk_of(mask_v, i, k)).then_inc(mask_in, 16)

            def load_res(i, k):
                sp.dma_start(xres[k % 2][:], chunk_of(x_v, i, k)).then_inc(res_in[k % 2], 16)

            def copy_q(c, g):
                wait_apart(sp, qh_ready, 4 * c + g + 1)
                wait_apart(sp, ql_ready, 4 * c + g + 1)
                for block_no, part in enumerate((q_hi, q_lo, q_hi)):
                    sp.dma_start(q_stack[D * block_no:D * block_no + D, HG * g:HG * g + HG, :].bitcast(F32),
                                 part[g % 2][:].bitcast(F32)).then_inc(q_in[g], 16)

            def load_adapter(k):
                a = sp.value_load(ids[k:k + 1].unsqueeze(0), min_val=0, max_val=ffn_w.shape[0] - 1)
                if k >= 2:
                    sp.wait_ge(s_wmix, 2 * (k - 1))
                sp.dma_start(w_raw[k % 2][:], ffn_v[bass.ds(a, 1)].rearrange(
                    "o p t d -> (o p) t d")).then_inc(s_w[k % 2], 16)
                sp.dma_start(b_rows[k:k + 1, :], ffn_b[bass.ds(a, 1), :]).then_inc(s_b, 16)

            sp.dma_start(ident_sb[:], eye[:, :]).then_inc(s_ident, 16)
            sp.dma_start(ctx_sb[:], ctx_in.rearrange("b p d -> p b d")).then_inc(s_ctx, 16)
            wkv_v = wkv.rearrange("(k p) n -> p k n", p=P)
            sp.dma_start(wkv_raw[:, :, 0:C], wkv_v[:, :, 0:C]).then_inc(s_wkv, 16)
            load_x(0, 0)
            sp.dma_start(wq_raw[:], wq.rearrange("(k p) n -> p k n", p=P)).then_inc(s_wq, 16)
            sp.dma_start(wkv_raw[:, :, C:2 * C], wkv_v[:, :, C:2 * C]).then_inc(s_wv, 16)
            load_mask(0, 0)
            sp.dma_start(gates[:, 0:1], g_attn.partition_broadcast(P)).then_inc(s_gates, 16)
            sp.dma_start(gates[:, 1:2], g_ffn.partition_broadcast(P)).then_inc(s_gates, 16)
            sp.dma_start(mix[:], weights.partition_broadcast(P)).then_inc(s_gates, 16)
            sp.dma_start(mix_rows[:], weights.rearrange("(k o) -> k o", o=1)).then_inc(s_gates, 16)
            sp.dma_start(bias_p[:], bproj.partition_broadcast(P)).then_inc(s_gates, 16)
            sp.dma_start(wp_raw[:], wproj.rearrange("(k p) n -> p k n", p=P)).then_inc(s_wp, 16)
            sp.wait_ge(mask_ready, 1)
            load_mask(0, 1)
            sp.wait_ge(xt_mm, 4)
            load_x(0, 1)
            load_adapter(0)
            sp.wait_ge(s_khi, KB)
            sp.wait_ge(s_klo, KB)
            for block_no, part in enumerate((k_hi, k_hi, k_lo)):
                sp.dma_start(k_stack[D * block_no:D * block_no + D, :, :, :].bitcast(F32),
                             part[:].bitcast(F32)).then_inc(s_kst, 16)
            sp.wait_ge(s_wqs, 2)
            for g in range(KB):
                copy_q(0, g)
                if g == 1:
                    load_adapter(1)
            for k in (2, 3, 4):
                load_adapter(k)

            def step(i, k, before=True, after=True, ahead=True):
                s = 2 * i + k
                for g in range(KB):
                    if not before:
                        for n in ((5,), (6, 7), (), ())[g]:
                            load_adapter(n)
                    if not before and g == 2:
                        sp.wait_ge(s_v, B)
                        load_res(0, 0)
                        sp.wait_ge(s_wpl, 1)
                        load_res(0, 1)
                    if g == 0 and ahead:
                        wait_apart(sp, xt_mm, 4 * s + 8)
                        load_x(i, k + 2)
                    if after:
                        wait_apart(sp, st_mm, UNITS * s + T * g + T)
                        copy_q(s + 1, g)
                    if g == 2 and ahead:
                        wait_apart(sp, mask_ready, s + 2)
                        load_mask(i, k + 2)
                    if before:
                        for t in ((), (0,), (1,), (2, 3))[g]:
                            wait_apart(sp, ffn_bank_read, 4 * s + t + 1)
                            sp.dma_start(chunk_of(out_v, i, k - 1)[:, t, :],
                                         xres[(k - 1) % 2][:, t, :]).then_inc(stored, 16)
                if before and after:
                    wait_apart(sp, stored, 64 * s)
                    load_res(i, k + 1)

            in_steps(sp, step)
            for t in range(T):
                sp.wait_ge(ffn_bank_read, 4 * LAST + 4 + t + 1)
                sp.dma_start(out_v[LAST % 2, LAST // 2][:, t, :], xres[AT_END][:, t, :]).then_inc(stored, 16)
            sp.wait_ge(stored, 64 * CHUNKS)

        @block.gpsimd
        def _(pool):
            def convert_mask(c, k):
                wait_apart(pool, mask_in, 16 * c + 16)
                nc.gpsimd.tensor_scalar(mask_bf[k % 2][:], mask_u8[:], MASKED, None,
                                        ALU.mult).then_inc(mask_ready, 1)

            def rstd_x(c):
                pool.wait_ge(stat1, 6 * c + 6)
                nc.gpsimd.tensor_tensor(rs1[:], ve1[:], m_half[:], ALU.pow).then_inc(rstd1, 1)

            def norm_x(c, t):
                wait_apart(pool, rstd1, c + 1)
                nc.gpsimd.tensor_scalar(xin[:, t, :], xin[:, t, :], nm1[:, t:t + 1],
                                        rs1[:, t:t + 1], ALU.add, ALU.mult).then_inc(xn_ready, 1)

            def divide(s, j):
                pool.wait_ge(inv_ready, UNITS * s + j + 1)
                nc.gpsimd.tensor_tensor(probs[j % 4][:, :, 0:M], probs[j % 4][:, :, 0:M],
                                        z_inv[:, j % 4, :].unsqueeze(2).to_broadcast([P, HG, M]),
                                        ALU.mult).then_inc(norm_ready, 1)

            def norm_h(f, t, at):
                pool.wait_ge(stat2, 3 * f + 3)
                nc.gpsimd.tensor_tensor(rs2[:, t:t + 1], ve2[:, t:t + 1], m_half[:, t:t + 1],
                                        ALU.pow).then_inc(rstd2, 1)
                wait_apart(pool, rstd2, f + 1)
                nc.gpsimd.tensor_scalar(x1n[t % 2][:], xres[at][:, t, :], nm2[:, t:t + 1],
                                        rs2[:, t:t + 1], ALU.add, ALU.mult).then_inc(h_ready, 1)

            def add_adapter_bias(f, t, at):
                pool.wait_ge(h_ready, f + 1)
                nc.gpsimd.tensor_tensor(xres[at][:, t, :], xres[at][:, t, :], bias_f[:],
                                        ALU.add).then_inc(x1b_ready, 1)

            nc.gpsimd.memset(m_half[:], -0.5).then_inc(setup_p, 1)
            pool.wait_ge(setup_p, 1)
            rstd_x(0)
            for t in range(T):
                norm_x(0, t)
            convert_mask(0, 0)
            rstd_x(1)
            for t in range(T):
                norm_x(1, t)
            divide(0, 0)

            def step(i, k, before=True, after=True, ahead=True):
                s = 2 * i + k

                def add_bias(t):
                    pool.wait_ge(res_in[k % 2], 16 * (i + k // 2) + 16)
                    if not before:
                        pool.wait_ge(setup_v, 2)
                    nc.gpsimd.tensor_tensor(xres[k % 2][:, t, :], xres[k % 2][:, t, :], bias_p[:],
                                            ALU.add).then_inc(res_ready, 1)

                for g in range(KB):
                    for p in range(T):
                        j = T * g + p
                        if in_range(j + 1, before, after):
                            divide(s, j + 1)
                        if p == 0 and g >= 1 and before:
                            add_bias(g - 1)
                        if (g, p) == (1, 1) and after:
                            if before:
                                pool.wait_ge(st_read, UNITS * s)
                            convert_mask(s + 1, k + 1)
                        if p == 2 and before:
                            norm_h(4 * s - 4 + g, g, (k - 1) % 2)
                        if p == 3 and before:
                            add_adapter_bias(4 * s - 4 + g, g, (k - 1) % 2)
                        if g == 3 and ahead:
                            if p == 0:
                                rstd_x(s + 2)
                            norm_x(s + 2, p)
                for t in range(T - 1 if before else 0, T):
                    add_bias(t)
                if not before:
                    pool.wait_ge(s_bf, 1)

            in_steps(pool, step)
            for t in range(T):
                if t >= 2:
                    pool.wait_ge(ht_mm, 4 * LAST + t - 1)
                norm_h(4 * LAST + t, t, AT_END)
                add_adapter_bias(4 * LAST + t, t, AT_END)

        @block.scalar
        def _(act):
            def xt_high(c, banks, tiles=range(T)):
                for t in tiles:
                    act.wait_ge(xt_mm, 4 * c + t + 1)
                    nc.scalar.copy(xn_hi[:, :, t * P:t * P + P],
                                   bank[banks[t]][:].rearrange("p (k n) -> p k n", k=KB)).then_inc(xt_hi, 1)

            def q_high(c, g, src):
                act.wait_ge(q_mm, 4 * c + g + 1)
                if g >= 2:
                    act.wait_ge(q_in[g - 2], REP * c + REP)
                elif not (isinstance(c, int) and c == 0):
                    act.wait_ge(q_in[g + 2], REP * c)
                nc.scalar.copy(q_hi[g % 2][:], bank[src][:]).then_inc(qh_ready, 1)

            def exponentials(s, j, first):
                act.wait_ge(st_read, UNITS * s + j + 1)
                if not (first and j < 4):
                    act.wait_ge(pt_mm, UNITS * s + j - 3)
                for h in range(HG):
                    last = nc.scalar.activation(probs[j % 4][:, h, :], scores[j % 2][:, h, :], ACT.Exp,
                                                bias=neg_max[:, j % 4, h:h + 1], scale=-1.0,
                                                accum_out=z_sum[:, j % 4, h:h + 1])
                last.then_inc(exp_ready, 1)

            def o_high(n, g, at):
                act.wait_ge(u_mm, 2 * n + 2)
                nc.scalar.copy(o_hi[at][:, g, :], bank[O_BANK][:]).then_inc(oh_ready, 1)

            def value(b):
                act.wait_ge(s_v_mm, b + 1)
                nc.scalar.copy(v_sb[:, b, :], bank[V_BANKS[b]][:]).then_inc(s_v, 1)

            def h_high(f, t, src):
                act.wait_ge(ht_mm, f + 1)
                nc.scalar.copy(h_hi[t % 2][:], bank[src][:].rearrange("p (k n) -> p k n", k=KB)).then_inc(ht_hi, 1)

            for b in range(B):
                act.wait_ge(s_ctxt_mm, b + 1)
                nc.scalar.copy(ctx_t[:, :, b * M:b * M + M],
                               bank[4 + b][:].rearrange("p (k n) -> p k n", k=KB)).then_inc(s_ctxt, 1)
            act.wait_ge(s_wkv, 16)
            for k in range(KB):
                last = nc.scalar.copy(wk_sb[:, k, :].rearrange("p (g d h) -> p g h d", h=HG, d=D),
                                      wkv_raw[:, k, 0:C].rearrange("p (g h d) -> p g h d", h=HG, d=D))
            last.then_inc(s_wk, 1)
            act.wait_ge(s_wq, 16)
            nc.scalar.copy(by_channel(wq_hi[:]), by_head(wq_raw[:])).then_inc(s_wqs, 1)
            xt_high(0, range(T))
            act.wait_ge(s_gates, 80)
            nc.scalar.activation(tanh_g[:], gates[:], ACT.Tanh).then_inc(s_tanh, 1)
            for g in range(KB):
                act.wait_ge(s_k_mm, g + 1)
                nc.scalar.copy(k_hi[:].rearrange("p (b g) m -> p g b m", b=B)[:, g],
                               bank[K_BANKS[g]][:, 0:B * M].rearrange("p (b m) -> p b m", b=B)).then_inc(s_khi, 1)
            for g in range(KB):
                q_high(0, g, g)
                if g == 1:
                    act.wait_ge(setup_v, 3)
                    nc.scalar.copy(wp_hi[:], wp_raw[:]).then_inc(s_wph, 1)
            value(0)
            exponentials(0, 0, True)
            exponentials(0, 1, True)
            value(1)

            def step(i, k, before=True, after=True, ahead=True):
                s = 2 * i + k

                def move_probs(j):
                    act.wait_ge(pt_mm, UNITS * s + j + 1)
                    if j % 2 == 0 and (before or j >= 4):
                        act.wait_ge(u_mm, UNITS // 2 * s + j // 2 - 1)
                    at = j % 2 * P
                    nc.scalar.copy(probs_t[j // 2 % 2][:, :, at:at + P], bank[PT_BANK[j % 2]][:].rearrange(
                        "p (h n) -> p h n", h=HG)).then_inc(pt_ready, 1)

                for g in range(KB):
                    for p in range(T):
                        j = T * g + p
                        if j == 0 and before:
                            o_high(KB * s - 1, KB - 1, (k - 1) % 2)
                        if j == 0 and after:
                            xt_high(s + 1, XT_BANKS, (0, 1))
                        if j == UNITS - 1 and before:
                            move_probs(j)
                            h_high(4 * s - 4 + g, g, FFN_BANK)
                        if in_range(j + 2, before, after):
                            exponentials(s, j + 2, not before)
                        if j == 0 and after:
                            xt_high(s + 1, XT_BANKS, (2, 3))
                        if j < UNITS - 1 or not before:
                            move_probs(j)
                        if p == 0 and g >= 1:
                            o_high(KB * s + g - 1, g - 1, k % 2)
                        if j == UNITS - 1 and not after:
                            o_high(KB * s + g, g, k % 2)
                        if p == 3 and before and g < 3:
                            h_high(4 * s - 4 + g, g, FFN_BANK)
                        if p == 3 and after:
                            q_high(s + 1, g, Q_BANK)
                        if not before and j == 11:
                            act.wait_ge(s_b_mm, 1)
                            nc.scalar.copy(bias_f[:], bank[BIAS_BANK][:]).then_inc(s_bf, 1)
                        if not before and g == 3:
                            act.wait_ge(s_wft_mm, p + 1)
                            nc.scalar.copy(wf_hi[:, p, :], bank[WF_BANKS[p]][:]).then_inc(s_wf, 1)

            in_steps(act, step)
            for t in range(T):
                h_high(4 * LAST + t, t, LAST_FFN_BANKS[t])

        @block.vector
        def _(dve):
            def stats_x(c, t):
                dve.wait_ge(x_in, 16 * c + 16)
                nc.vector.bn_stats(bn1[:, t, :], xin[:, t, :]).then_inc(stat1, 1)
                if t == T - 1:
                    wait_apart(dve, stat1, 6 * c + 4)
                    for u in range(T):
                        last = nc.vector.bn_aggr(mv1[:, u, :], bn1[:, u, :])
                    last.then_inc(stat1, 1)
                    dve.wait_ge(stat1, 6 * c + 5)
                    nc.vector.tensor_scalar(nm1[:], mv1[:, :, 0], -1.0, None, ALU.mult)
                    nc.vector.tensor_scalar(ve1[:], mv1[:, :, 1], EPS, None, ALU.add).then_inc(stat1, 1)

            def xt_low(c, banks, tiles=range(T)):
                for t in tiles:
                    dve.wait_ge(xt_hi, 4 * c + t + 1)
                    part = slice(t * P, t * P + P)
                    nc.vector.tensor_tensor(xn_lo[:, :, part], bank[banks[t]][:].rearrange("p (k n) -> p k n", k=KB),
                                            xn_hi[:, :, part].bitcast(F32), ALU.subtract).then_inc(xt_lo, 1)

            def q_low(c, g, src):
                dve.wait_ge(qh_ready, 4 * c + g + 1)
                nc.vector.tensor_tensor(q_lo[g % 2][:], bank[src][:], q_hi[g % 2][:].bitcast(F32),
                                        ALU.subtract).then_inc(ql_ready, 1)

            def mask_scores(s, k, j, first):
                c = j // UNITS
                wait_apart(dve, mask_ready, s + c + 1)
                wait_apart(dve, st_mm, UNITS * s + j + 1)
                if not (first and j < 2):
                    wait_apart(dve, exp_ready, UNITS * s + j - 1)
                for h in range(HG):
                    last = nc.vector.tensor_tensor_reduce(
                        out=scores[j % 2][:, h, 0:M], in0=bank[S_BANK[j % 2]][:, h * M:h * M + M],
                        in1=mask_bf[(k + c) % 2][:, j % T, :], scale=-SCALE, scalar=0.0,
                        op0=ALU.add, op1=ALU.min, accum_out=neg_max[:, j % 4, h:h + 1])
                last.then_inc(st_read, 1)

            def invert(s, j):
                dve.wait_ge(exp_ready, UNITS * s + j + 1)
                nc.vector.reciprocal(z_inv[:, j % 4, :], z_sum[:, j % 4, :]).then_inc(inv_ready, 1)

            def mix_adapter(k, half):
                blocks = slice(half * KB // 2, (half + 1) * KB // 2)
                flat = lambda a: a[:, blocks, :].rearrange("p k n -> p (k n)")
                if half == 0:
                    dve.wait_ge(s_w[k % 2], 16 * (k // 2) + 16)
                    if k == 0:
                        dve.wait_ge(setup_v, 1)
                    else:
                        dve.wait_ge(s_wmix, 2 * k)
                if k == 0:
                    last = nc.vector.tensor_scalar(flat(w_acc), flat(w_raw[0]), mix[:, 0:1], None, ALU.mult)
                else:
                    last = nc.vector.scalar_tensor_tensor(
                        out=flat(w_acc), in0=flat(w_raw[k % 2]), scalar=mix[:, k:k + 1],
                        in1=flat(w_acc), op0=ALU.mult, op1=ALU.add)
                last.then_inc(s_wmix, 1)

            def o_low(n, g, at):
                dve.wait_ge(oh_ready, n + 1)
                nc.vector.tensor_tensor(o_lo[at][:, g, :], bank[O_BANK][:], o_hi[at][:, g, :].bitcast(F32),
                                        ALU.subtract).then_inc(ol_ready, 1)

            def add_x1(f, t, at, src):
                xr = xres[at][:, t, :]
                dve.wait_ge(pj_mm, f + 1)
                dve.wait_ge(res_ready, f + 1)
                nc.vector.tensor_tensor(xr, bank[src][:], xr, ALU.add).then_inc(x1_ready, 1)
                dve.wait_ge(x1_ready, f + 1)
                nc.vector.bn_stats(bn2[:, t, :], xr).then_inc(stat2, 1)
                wait_apart(dve, stat2, 3 * f + 1)
                nc.vector.bn_aggr(mv2[:, t, :], bn2[:, t, :]).then_inc(stat2, 1)
                dve.wait_ge(stat2, 3 * f + 2)
                nc.vector.tensor_scalar(nm2[:, t:t + 1], mv2[:, t, 0:1], -1.0, None, ALU.mult)
                nc.vector.tensor_scalar(ve2[:, t:t + 1], mv2[:, t, 1:2], EPS, None, ALU.add).then_inc(stat2, 1)

            def h_low(f, t, src):
                dve.wait_ge(ht_hi, f + 1)
                nc.vector.tensor_tensor(h_lo[t % 2][:], bank[src][:].rearrange("p (k n) -> p k n", k=KB),
                                        h_hi[t % 2][:].bitcast(F32), ALU.subtract).then_inc(ht_lo, 1)

            def add_output(f, t, at, src):
                dve.wait_ge(ff_mm, f + 1)
                dve.wait_ge(x1b_ready, f + 1)
                nc.vector.tensor_tensor(xres[at][:, t, :], bank[src][:], xres[at][:, t, :],
                                        ALU.add).then_inc(ffn_bank_read, 1)

            for i in range(2):
                nc.vector.memset(scores[i][:, :, M:M + 1], 0.0)
            for t in range(T):
                stats_x(0, t)
            dve.wait_ge(s_wqs, 1)
            nc.vector.tensor_tensor(by_channel(wq_lo[:]), by_head(wq_raw[:]), by_channel(wq_hi[:].bitcast(F32)),
                                    ALU.subtract).then_inc(s_wqs, 1)
            xt_low(0, range(T))
            for g in range(KB):
                dve.wait_ge(s_khi, g + 1)
                nc.vector.tensor_tensor(k_lo[:].rearrange("p (b g) m -> p g b m", b=B)[:, g],
                                        bank[K_BANKS[g]][:, 0:B * M].rearrange("p (b m) -> p b m", b=B),
                                        k_hi[:].bitcast(F32).rearrange("p (b g) m -> p g b m", b=B)[:, g],
                                        ALU.subtract).then_inc(s_klo, 1)
            dve.wait_ge(s_tanh, 1)
            nc.vector.tensor_scalar(mix[:], mix[:], tanh_g[:, 1:2], None, ALU.mult).then_inc(setup_v, 1)
            nc.vector.tensor_scalar(mix_cols[:], mix_rows[:].to_broadcast([NK, P]), tanh_g[0:NK, 1:2], None, ALU.mult)
            nc.vector.tensor_scalar(bias_p[:], bias_p[:], tanh_g[:, 0:1], None, ALU.mult).then_inc(setup_v, 1)
            dve.wait_ge(s_wp, 16)
            nc.vector.tensor_scalar(wp_raw[:], wp_raw[:], tanh_g[:, 0:1], None, ALU.mult).then_inc(setup_v, 1)
            q_low(0, 0, 0)
            for t in range(T):
                stats_x(1, t)
            q_low(0, 1, 1)
            mix_adapter(0, 0)
            mix_adapter(0, 1)
            dve.wait_ge(s_wph, 1)
            nc.vector.tensor_tensor(wp_lo[:], wp_raw[:], wp_hi[:].bitcast(F32), ALU.subtract).then_inc(s_wpl, 1)
            q_low(0, 2, 2)
            q_low(0, 3, 3)
            mask_scores(0, 0, 0, True)
            mask_scores(0, 0, 1, True)
            invert(0, 0)
            mask_scores(0, 0, 2, True)
            invert(0, 1)
            mix_adapter(1, 0)
            mix_adapter(1, 1)

            def step(i, k, before=True, after=True, ahead=True):
                s = 2 * i + k
                f, at = 4 * s - 4, (k - 1) % 2

                for g in range(KB):
                    for p in range(T):
                        j = T * g + p
                        if j == 0 and before:
                            o_low(KB * s - 1, KB - 1, (k - 1) % 2)
                        if j == 0 and after:
                            xt_low(s + 1, XT_BANKS, (0, 1))
                        if in_range(j + 3, before, after):
                            mask_scores(s, k, j + 3, not before)
                        if p == 0 and g >= 1:
                            o_low(KB * s + g - 1, g - 1, k % 2)
                        if j == 0 and after:
                            xt_low(s + 1, XT_BANKS, (2, 3))
                        if g == 2 and ahead:
                            stats_x(s + 2, p)
                        if j == UNITS - 1 and before:
                            h_low(f + g, g, FFN_BANK)
                        if in_range(j + 2, before, after):
                            invert(s, j + 2)
                        if p == 1 and before:
                            add_x1(f + g, g, at, PROJ_BANK)
                        if not before and g < 3:
                            mix_adapter(2 + 2 * g + p // 2, p % 2)
                        if not before and g == 3:
                            dve.wait_ge(s_wf, p + 1)
                            nc.vector.tensor_tensor(wf_lo[:, p, :], bank[WF_BANKS[p]][:], wf_hi[:, p, :].bitcast(F32),
                                                    ALU.subtract).then_inc(ffn_bank_read, 1)
                        if p == 2 and before and g >= 1:
                            add_output(f + g - 1, g - 1, at, FFN_BANK)
                        if p == 3 and before and g < 3:
                            h_low(f + g, g, FFN_BANK)
                        if p == 3 and after:
                            q_low(s + 1, g, Q_BANK)
                if before:
                    if not after:
                        o_low(KB * s + KB - 1, KB - 1, k % 2)
                    add_output(f + T - 1, T - 1, at, FFN_BANK)

            in_steps(dve, step)
            f = 4 * LAST
            for t in range(T):
                if t == 3:
                    h_low(f, 0, LAST_FFN_BANKS[0])
                add_x1(f + t, t, AT_END, LAST_PROJ_BANKS[t])
            h_low(f + 1, 1, LAST_FFN_BANKS[1])
            for t in range(2, T):
                add_output(f + t - 2, t - 2, AT_END, LAST_FFN_BANKS[t - 2])
                h_low(f + t, t, LAST_FFN_BANKS[t])
            for t in range(2, T):
                add_output(f + t, t, AT_END, LAST_FFN_BANKS[t])

        @block.tensor
        def _(pe):
            mm = nc.tensor.matmul

            def split_product(dst, lhs_h, lhs_l, rhs_h, rhs_l, blocks=range(KB)):
                for k in blocks:
                    mm(dst, lhs_h(k), rhs_h(k), start=(k == 0), stop=False)
                    mm(dst, lhs_h(k), rhs_l(k), start=False, stop=False)
                    last = mm(dst, lhs_l(k), rhs_h(k), start=False, stop=(k == KB - 1))
                return last

            def transpose_x(c, t, dst):
                pe.wait_ge(xn_ready, 4 * c + t + 1)
                for k in range(KB):
                    last = nc.tensor.transpose(bank[dst][:, k * P:k * P + P], xin[:, t, k * P:k * P + P], ident)
                last.then_inc(xt_mm, 1)

            def queries(g, dst, blocks=range(KB)):
                cols = slice(g * P, g * P + P)
                return split_product(bank[dst][:], lambda k: wq_hi[:, k, cols], lambda k: wq_lo[:, k, cols],
                                     lambda k: xn_hi[:, k, :], lambda k: xn_lo[:, k, :], blocks)

            def unit_scores(s, k, j, first):
                c, g, t = j // UNITS, j % UNITS // T, j % T
                if t == 0:
                    pe.wait_ge(q_in[g], REP * (s + c) + REP)
                if not (first and j < 2):
                    pe.wait_ge(st_read, UNITS * s + j - 1)
                for h in range(HG):
                    last = mm(bank[S_BANK[j % 2]][:, h * M:h * M + M],
                              q_stack[0:KROWS, HG * g + h, t * P:t * P + P],
                              k_stack[0:KROWS, h, (k + c) % 2 * KB + g, :], start=True, stop=True)
                last.then_inc(st_mm, 1)

            def products(units, groups, k, j, first):
                c, g, t = j // UNITS, j % UNITS // T, j % T
                pe.wait_ge(pt_ready, units + j + 2)
                if t == 0 and not first:
                    pe.wait_ge(ol_ready, groups + j // T)
                for h in range(HG):
                    at = D * (HG * g + h)
                    last = mm(bank[O_BANK][D * h:D * h + D, t * P:(t + 2) * P],
                              v_sb[:, (k + c) % 2, at:at + D], probs_t[j // 2 % 2][:, h, :],
                              start=True, stop=True, skip_group_check=True)
                last.then_inc(u_mm, 1)

            def project(at, t, dst, blocks=range(KB)):
                part = slice(t * P, t * P + P)
                return split_product(bank[dst][:], lambda q: o_hi[at][:, q, part], lambda q: o_lo[at][:, q, part],
                                     lambda q: wp_hi[:, q, :], lambda q: wp_lo[:, q, :], blocks)

            def transpose_h(f, t, dst):
                pe.wait_ge(h_ready, f + 1)
                for q in range(KB):
                    last = nc.tensor.transpose(bank[dst][:, q * P:q * P + P], x1n[t % 2][:, q * P:q * P + P], ident)
                last.then_inc(ht_mm, 1)

            def adapt(f, t, dst):
                pe.wait_ge(ht_lo, f + 1)
                split_product(bank[dst][:], lambda q: h_hi[t % 2][:, q, :], lambda q: h_lo[t % 2][:, q, :],
                              lambda q: wf_hi[:, q, :], lambda q: wf_lo[:, q, :]).then_inc(ff_mm, 1)

            pe.wait_ge(s_ident, 16)
            pe.wait_ge(s_ctx, 16)
            for b in range(B):
                for k in range(KB):
                    last = nc.tensor.transpose(bank[4 + b][:, k * P:k * P + P], ctx_sb[:, b, k * P:k * P + P], ident)
                last.then_inc(s_ctxt_mm, 1)

            def keys(g):
                for k in range(KB):
                    last = mm(bank[K_BANKS[g]][:, 0:B * M],
                              wk_sb[:, k, g * P:g * P + P], ctx_t[:, k, :],
                              start=(k == 0), stop=(k == KB - 1))
                last.then_inc(s_k_mm, 1)

            pe.wait_ge(s_wk, 1)
            pe.wait_ge(s_ctxt, B)
            keys(0)
            keys(1)
            for t in range(T):
                transpose_x(0, t, t)
            keys(2)
            keys(3)

            def values(b):
                for k in range(KB):
                    last = mm(bank[V_BANKS[b]][:], ctx_t[:, k, b * M:b * M + M], wkv_raw[:, k, C:2 * C],
                              start=(k == 0), stop=(k == KB - 1))
                last.then_inc(s_v_mm, 1)

            pe.wait_ge(s_wqs, 2)
            for g in range(KB):
                pe.wait_ge(xt_lo, 4)
                queries(g, g).then_inc(q_mm, 1)
            pe.wait_ge(s_wv, 16)
            pe.wait_ge(s_klo, KB)
            values(0)
            pe.wait_ge(s_kst, 16 * 3)
            pe.wait_ge(ql_ready, 2)
            unit_scores(0, 0, 0, True)
            unit_scores(0, 0, 1, True)
            values(1)
            unit_scores(0, 0, 2, True)
            pe.wait_ge(ql_ready, 4)
            pe.wait_ge(s_v, 1)

            def step(i, k, before=True, after=True, ahead=True):
                s = 2 * i + k

                def transpose_probs(j):
                    pe.wait_ge(norm_ready, UNITS * s + j + 1)
                    if before or j >= 2:
                        pe.wait_ge(pt_ready, UNITS * s + j - 1)
                    for h in range(HG):
                        last = nc.tensor.transpose(bank[PT_BANK[j % 2]][:, h * P:h * P + P],
                                                   probs[j % 4][:, h, 0:M], ident)
                    last.then_inc(pt_mm, 1)

                for g in range(KB):
                    f = 4 * s - 4 + g
                    for p in range(T):
                        j = T * g + p
                        if j == 0 and before:
                            products(UNITS * s, KB * s, k, -2, False)
                        if in_range(j + 3, before, after):
                            unit_scores(s, k, j + 3, not before)
                        transpose_probs(j)
                        if j % 2 == 0 and j >= 2:
                            products(UNITS * s, KB * s, k, j - 2, not before and j == 2)
                        if j == 0:
                            if after:
                                if before:
                                    pe.wait_ge(ffn_bank_read, 4 * s)
                                pe.wait_ge(ql_ready, 4 * s + 4)
                                transpose_x(s + 1, 0, XT_BANKS[0])
                                transpose_x(s + 1, 1, XT_BANKS[1])
                            if before:
                                pe.wait_ge(ol_ready, KB * s)
                                pe.wait_ge(s_wpl, 1)
                                project((k - 1) % 2, g, PROJ_BANK, range(KB // 2))
                            if after:
                                for t in (2, 3):
                                    pe.wait_ge(xt_lo, 4 * s + 4 + t - 1)
                                    transpose_x(s + 1, t, XT_BANKS[t])
                            if before:
                                project((k - 1) % 2, g, PROJ_BANK, range(KB // 2, KB)).then_inc(pj_mm, 1)
                        elif p == 0 and before:
                            pe.wait_ge(x1_ready, f)
                            project((k - 1) % 2, g, PROJ_BANK).then_inc(pj_mm, 1)
                        if g == 0 and p >= 1 and after:
                            if p == 1:
                                pe.wait_ge(xt_lo, 4 * s + 8)
                            last = queries(g, Q_BANK, Q_BLOCKS[g][p])
                            if p == 3:
                                last.then_inc(q_mm, 1)
                        if g >= 1 and p == 1 and before:
                            adapt(f - 1, g - 1, FFN_BANK)
                        if g >= 1 and p == 2 and after:
                            pe.wait_ge(ql_ready, 4 * s + 4 + g)
                            queries(g, Q_BANK, Q_BLOCKS[g][p])
                        if p == 3 and before:
                            pe.wait_ge(ffn_bank_read, 4 * s + g)
                            transpose_h(f, g, FFN_BANK)
                        if g >= 1 and p == 3 and after:
                            queries(g, Q_BANK, Q_BLOCKS[g][p]).then_inc(q_mm, 1)
                        if j == UNITS - 1 and not after:
                            products(UNITS * s, KB * s, k, UNITS - 2, False)
                        if g == T - 1 and p == 3 and before:
                            adapt(f, g, FFN_BANK)
                        if not before and j == 11:
                            pe.wait_ge(s_b, 16 * NK)
                            mm(bank[BIAS_BANK][:], mix_cols[:], b_rows[:], start=True, stop=True).then_inc(s_b_mm, 1)
                        if not before and (g, p) == (3, 1):
                            pe.wait_ge(s_bf, 1)
                        if not before and g == 3:
                            if p == 0:
                                pe.wait_ge(s_wmix, 2 * NK)
                            if p >= 2:
                                pe.wait_ge(ffn_bank_read, p - 1)
                            for o in range(KB):
                                last = nc.tensor.transpose(bank[WF_BANKS[p]][:, o * P:o * P + P],
                                                           w_acc[:, o, p * P:p * P + P], ident)
                            last.then_inc(s_wft_mm, 1)

            in_steps(pe, step)
            f, ffn_bank = 4 * LAST, LAST_FFN_BANKS
            pe.wait_ge(ol_ready, KB * CHUNKS)
            for t in range(3):
                project(AT_END, t, LAST_PROJ_BANKS[t]).then_inc(pj_mm, 1)
            transpose_h(f, 0, ffn_bank[0])
            project(AT_END, 3, LAST_PROJ_BANKS[3]).then_inc(pj_mm, 1)
            transpose_h(f + 1, 1, ffn_bank[1])
            for t in range(2, T):
                adapt(f + t - 2, t - 2, ffn_bank[t - 2])
                transpose_h(f + t, t, ffn_bank[t])
            for t in range(2, T):
                adapt(f + t, t, ffn_bank[t])


_INS = ['x', 'ctx_1024', 'mask_BxSxS2_bk0', 'g_xattn', 'g_ffn', 'L0_xattn_Wq', 'L0_xattn_Wkv',
        'L0_xattn_Wproj', 'L0_xattn_bproj', 'L0_ffn_W', 'L0_ffn_b', 'L0_ffn_ids', 'L0_ffn_weights']


def kernel(**inputs):
    import concourse.bacc as bacc
    from concourse.bass_utils import run_bass_kernel_spmd

    nc = bacc.Bacc("TRN2", target_bir_lowering=False, num_devices=1, dynamic_dma_scratch_size=64)
    arrays, args = {}, []

    def add(name, a):
        arrays[name] = a
        args.append(nc.dram_tensor(name, a.shape, mybir.dt.from_np(a.dtype), kind="ExternalInput").ap())

    for name in _INS:
        a = np.ascontiguousarray(inputs[name])
        add(f"in_{name}", a)
    add("const_f32", np.eye(128, dtype=np.float32))
    shape = inputs['x'].shape
    args.append(nc.dram_tensor("out_0", shape, mybir.dt.float32, kind="ExternalOutput").ap())
    flamingo_program(nc, *args)
    r = run_bass_kernel_spmd(nc, [arrays], core_ids=[0])
    return r.results[0]["out_0"]
```
